# Optimizing a Trainium2 kernel written in Bass

```python
import numpy as np
import jax
import jax.numpy as jnp

def _softmax(x, axis=-1):
    return jax.nn.softmax(x, axis=axis)

def _gelu(x):
    return jax.nn.gelu(x, approximate=True)

def _silu(x):
    return jax.nn.silu(x)

def _sigmoid(x):
    return jax.nn.sigmoid(x)

def _layernorm(x, axis=-1, eps=1e-05):
    m = jnp.mean(x, axis=axis, keepdims=True)
    v = jnp.var(x, axis=axis, keepdims=True)
    return (x - m) / jnp.sqrt(v + eps)

def _scatter_add(tgt, idx, src, axis=0):
    return tgt.at[idx].add(src)

def _segment_sum(src, seg, n):
    return jax.ops.segment_sum(src, seg, n)
kernel_name = 'mk_gnn_resnorm_d2_gnn_r32_af735c'

def setup_inputs(seed: int=0):
    np.random.seed(seed)
    _w = jnp.asarray

    def _rec_inputs():
        import jax
        import jax.numpy as jnp
        _gk = jax.random.key(seed)
        x = -0.000202 + 1 * jax.random.normal(jax.random.fold_in(_gk, 1), (3125, 128), jnp.float32)
        _s = jax.random.randint(jax.random.fold_in(_gk, 2), (25000,), 0, 3125, jnp.int32)
        _d = jax.random.randint(jax.random.fold_in(_gk, 3), (25000,), 0, 3125, jnp.int32)
        _loop = jnp.arange(3125, dtype=jnp.int32)
        src = jnp.concatenate([_s, _d, _loop])
        dst = jnp.concatenate([_d, _s, _loop])
        _o = jnp.argsort(dst, stable=True)
        src = src[_o]
        dst = dst[_o]
        edge_attr_16 = -0.00010739 + 0.99994 * jax.random.normal(jax.random.fold_in(_gk, 12), (53125, 16), jnp.float32)
        return (x, src, dst, edge_attr_16)
    x, src, dst, edge_attr_16 = _rec_inputs()

    def _L0_gnn_setup():
        import jax, jax.numpy as jnp
        import numpy as np
        BN_EPS = 0.001
        D = 128
        EDGE_DIM = 16
        N_NODES = 50000
        N_EDGES = 25000

        def _bn(x, gamma, beta, mean, var):
            return (x - mean) * jax.lax.rsqrt(var + BN_EPS) * gamma + beta
        key = jax.random.key(seed)
        ks = jax.random.split(key, 12)
        inp = {'node_feat': jax.random.normal(ks[0], (N_NODES, D), jnp.float32), 'edge_feat': jax.random.normal(ks[1], (N_EDGES, EDGE_DIM), jnp.float32), 'src': jax.random.randint(ks[2], (N_EDGES,), 0, N_NODES, jnp.int32), 'dst': jax.random.randint(ks[3], (N_EDGES,), 0, N_NODES, jnp.int32), 'We1': jax.random.normal(ks[4], (EDGE_DIM, 2 * D), jnp.float32) * 0.05, 'be1': jnp.zeros((2 * D,), jnp.float32), 'We2': jax.random.normal(ks[5], (2 * D, D), jnp.float32) * 0.05, 'be2': jnp.zeros((D,), jnp.float32), 'eps': jax.random.normal(ks[6], (1,), jnp.float32) * 0.05, 'Wm1': jax.random.normal(ks[7], (D, 2 * D), jnp.float32) * 0.05, 'bm1': jnp.zeros((2 * D,), jnp.float32), 'g1': jnp.ones((2 * D,), jnp.float32), 'b1': jnp.zeros((2 * D,), jnp.float32), 'm1': jnp.zeros((2 * D,), jnp.float32), 'v1': jnp.ones((2 * D,), jnp.float32), 'Wm2': jax.random.normal(ks[8], (2 * D, D), jnp.float32) * 0.05, 'bm2': jnp.zeros((D,), jnp.float32), 'g2': jnp.ones((D,), jnp.float32), 'b2': jnp.zeros((D,), jnp.float32), 'm2': jnp.zeros((D,), jnp.float32), 'v2': jnp.ones((D,), jnp.float32)}
        return inp
    _L0_gnn_all = _L0_gnn_setup()
    _L0_gnn_in = {k: v for k, v in _L0_gnn_all.items() if k in ('We1', 'be1', 'We2', 'be2', 'eps', 'Wm1', 'bm1', 'g1', 'b1', 'm1', 'v1', 'Wm2', 'bm2', 'g2', 'b2', 'm2', 'v2')}
    del _L0_gnn_all

    def _L1_gnn_setup():
        import jax, jax.numpy as jnp
        import numpy as np
        N_NODES = 50000
        N_EDGES = 25000
        D = 128
        key = jax.random.key(seed)
        ks = jax.random.split(key, 7)
        return {'shape_features': jax.random.normal(ks[0], (N_NODES, D), dtype=jnp.float32), 'W1': jax.random.normal(ks[1], (D, D), dtype=jnp.float32) * 0.05, 'b1': jax.random.normal(ks[2], (D,), dtype=jnp.float32) * 0.05, 'W2': jax.random.normal(ks[3], (D, D), dtype=jnp.float32) * 0.05, 'b2': jax.random.normal(ks[4], (D,), dtype=jnp.float32) * 0.05, 'edge_src': jax.random.randint(ks[5], (N_EDGES,), 0, N_NODES, dtype=jnp.int32), 'edge_dst': jax.random.randint(ks[6], (N_EDGES,), 0, N_NODES, dtype=jnp.int32)}
    _L1_gnn_all = _L1_gnn_setup()
    _L1_gnn_in = {k: v for k, v in _L1_gnn_all.items() if k in ('W1', 'b1', 'W2', 'b2')}
    del _L1_gnn_all
    return {'x': x, 'src': src, 'dst': dst, 'edge_attr_16': edge_attr_16, 'L0_gnn_We1': _L0_gnn_in['We1'], 'L0_gnn_be1': _L0_gnn_in['be1'], 'L0_gnn_We2': _L0_gnn_in['We2'], 'L0_gnn_be2': _L0_gnn_in['be2'], 'L0_gnn_eps': _L0_gnn_in['eps'], 'L0_gnn_Wm1': _L0_gnn_in['Wm1'], 'L0_gnn_bm1': _L0_gnn_in['bm1'], 'L0_gnn_g1': _L0_gnn_in['g1'], 'L0_gnn_b1': _L0_gnn_in['b1'], 'L0_gnn_m1': _L0_gnn_in['m1'], 'L0_gnn_v1': _L0_gnn_in['v1'], 'L0_gnn_Wm2': _L0_gnn_in['Wm2'], 'L0_gnn_bm2': _L0_gnn_in['bm2'], 'L0_gnn_g2': _L0_gnn_in['g2'], 'L0_gnn_b2': _L0_gnn_in['b2'], 'L0_gnn_m2': _L0_gnn_in['m2'], 'L0_gnn_v2': _L0_gnn_in['v2'], 'L1_gnn_W1': _L1_gnn_in['W1'], 'L1_gnn_b1': _L1_gnn_in['b1'], 'L1_gnn_W2': _L1_gnn_in['W2'], 'L1_gnn_b2': _L1_gnn_in['b2']}

def reference(x, src, dst, edge_attr_16, L0_gnn_We1, L0_gnn_be1, L0_gnn_We2, L0_gnn_be2, L0_gnn_eps, L0_gnn_Wm1, L0_gnn_bm1, L0_gnn_g1, L0_gnn_b1, L0_gnn_m1, L0_gnn_v1, L0_gnn_Wm2, L0_gnn_bm2, L0_gnn_g2, L0_gnn_b2, L0_gnn_m2, L0_gnn_v2, L1_gnn_W1, L1_gnn_b1, L1_gnn_W2, L1_gnn_b2):
    import jax
    import jax.numpy as jnp

    def _L0_gnn_ref(node_feat, edge_feat, src, dst, We1, be1, We2, be2, eps, Wm1, bm1, g1, b1, m1, v1, Wm2, bm2, g2, b2, m2, v2):
        import jax, jax.numpy as jnp
        import numpy as np
        BN_EPS = 0.001
        D = 128
        EDGE_DIM = 16
        N_NODES = 50000
        N_EDGES = 25000

        def _bn(x, gamma, beta, mean, var):
            return (x - mean) * jax.lax.rsqrt(var + BN_EPS) * gamma + beta
        e = (edge_feat @ We1 + be1) @ We2 + be2
        msg = jax.nn.relu(e + node_feat[src])
        pooled = jax.ops.segment_sum(msg, dst, num_segments=node_feat.shape[0])
        h = (1.0 + eps) * node_feat + pooled
        h = jax.nn.relu(_bn(h @ Wm1 + bm1, g1, b1, m1, v1)) @ Wm2 + bm2
        return _bn(h, g2, b2, m2, v2)

    def _L1_gnn_ref(shape_features, W1, b1, W2, b2, edge_src, edge_dst):
        import jax, jax.numpy as jnp
        import numpy as np
        N_NODES = 50000
        N_EDGES = 25000
        D = 128
        out1 = jnp.einsum('nd,od->no', shape_features, W1) + b1
        aggr = jax.ops.segment_sum(shape_features[edge_src], edge_dst, num_segments=shape_features.shape[0])
        return out1 + jnp.einsum('nd,od->no', aggr, W2) + b2
    x = _layernorm(x + _L0_gnn_ref(x, edge_attr_16, src, dst, L0_gnn_We1, L0_gnn_be1, L0_gnn_We2, L0_gnn_be2, L0_gnn_eps, L0_gnn_Wm1, L0_gnn_bm1, L0_gnn_g1, L0_gnn_b1, L0_gnn_m1, L0_gnn_v1, L0_gnn_Wm2, L0_gnn_bm2, L0_gnn_g2, L0_gnn_b2, L0_gnn_m2, L0_gnn_v2), axis=-1)
    x = _layernorm(x + _L1_gnn_ref(x, L1_gnn_W1, L1_gnn_b1, L1_gnn_W2, L1_gnn_b2, src, dst), axis=-1)
    return x

_drawn_inputs = setup_inputs


def setup_inputs(seed=0):
    import zlib

    import numpy as np

    out = dict(_drawn_inputs(seed))
    spreads = {'L0_gnn_be1': (0.0, 0.1),
     'L0_gnn_be2': (0.0, 0.1),
     'L0_gnn_bm1': (0.0, 0.468),
     'L0_gnn_g1': (1.0, 0.2),
     'L0_gnn_b1': (0.0, 0.322),
     'L0_gnn_m1': (0.0, 0.339),
     'L0_gnn_v1': (1.0, 0.2),
     'L0_gnn_bm2': (0.0, 0.314),
     'L0_gnn_g2': (1.0, 0.2),
     'L0_gnn_b2': (0.0, 0.388),
     'L0_gnn_m2': (0.0, 0.379),
     'L0_gnn_v2': (1.0, 0.2)}
    factors = {'edge_attr_16': 3.008, 'L0_gnn_We1': 2.984, 'L1_gnn_b1': 8.0, 'L1_gnn_b2': 8.0}
    for name, (base, spread) in spreads.items():
        noise = np.random.default_rng([zlib.crc32(name.encode()), seed]).standard_normal(out[name].shape)
        drawn = base * np.exp(spread * noise) if base else spread * noise
        out[name] = jnp.asarray(drawn.astype(out[name].dtype))
    for name, factor in factors.items():
        out[name] = (out[name] * factor).astype(out[name].dtype)
    return out
```

```python
from contextlib import ExitStack

import concourse.bass as bass
from concourse import mybir

F32 = mybir.dt.float32
I32 = mybir.dt.int32
ALU = mybir.AluOpType
ACT = mybir.ActivationFunctionType

NODES, D, HID, EF = 3125, 128, 256, 16
EDGES = 53125
TILE = 128
GROUP = 4
GROUPS = -(-EDGES // (TILE * GROUP))
TILES = GROUPS * GROUP
BLOCK = 125
BLOCKS = NODES // BLOCK
SPAN = 5
SUPERS = BLOCKS // SPAN
SNODES = SPAN * BLOCK
LOW = 3
BANK = 512
HALVES = HID // 128
BN_EPS, LN_EPS = 0.001, 1e-05


def gnn_kernel(nc, x, xT, src_t, dst_t, efT, We1T, We2, be2, eps, Wm1, bm1, g1, b1, m1, v1,
               Wm2, bm2, g2, b2, m2, v2, W1T, bb1, W2T, bb2, out, x1_dram):
    with ExitStack() as ctx:
        def sb(name, shape, dt=F32):
            return ctx.enter_context(nc.sbuf_tensor(name, shape, dt))

        def sem(name):
            return ctx.enter_context(nc.semaphore(name))

        ps = ctx.enter_context(nc.psum_tensor("ps", [128, 8 * BANK], F32))

        we1T = sb("we1T", [128, HALVES, EF + 1])
        we2 = sb("we2", [128, HALVES, D])
        be2_row = sb("be2_row", [1, D])
        unit_row = sb("unit_row", [1, EF + 1])
        wc = sb("wc", [EF + 1, D])
        wm1 = sb("wm1", [128, HID])
        wm2 = sb("wm2", [128, HALVES, D])
        w1T = sb("w1T", [128, D])
        w2T = sb("w2T", [128, D])
        bn1 = sb("bn1", [128, 5, HALVES])
        bn2 = sb("bn2", [128, 5, D])
        outb = sb("outb", [128, 2, D])
        tmp1 = sb("tmp1", [128, 4, HALVES])
        scale1 = sb("scale1", [128, HALVES])
        bias1 = sb("bias1", [128, HALVES])
        tmp2 = sb("tmp2", [128, 4, D])
        scale2 = sb("scale2", [128, D])
        bias2 = sb("bias2", [128, D])
        biasO = sb("biasO", [128, D])
        eps1 = sb("eps1", [128, 1])
        eps1p = sb("eps1p", [128, 1])
        epsc = sb("epsc", [128, 2])
        ident = sb("ident", [128, 128])
        zeros = sb("zeros", [128, 128])
        node_iota = sb("node_iota", [128, NODES])
        dst_i = sb("dst_i", [128, TILES], I32)
        dst_f = sb("dst_f", [128, TILES])

        hT = sb("hT", [128, NODES])
        x1T = sb("x1T", [128, NODES])
        x1 = sb("x1", [BLOCK, BLOCKS, D])
        x_in = sb("x_in", [BLOCK, BLOCKS, D])

        idx = sb("idx", [128, GROUP], I32)
        ef = sb("ef", [EF + 1, GROUP * TILE])
        gath = sb("gath", [128, GROUP, D])
        summed = sb("summed", [128, GROUP, D])
        msg = sb("msg", [128, GROUP, D])
        hot = sb("hot", [128, NODES])

        rT = sb("rT", [128, HALVES, SNODES])
        y = sb("y", [BLOCK, SPAN, D])
        stats = sb("stats", [BLOCK, SPAN, 6])
        mv = sb("mv", [BLOCK, SPAN, 2])
        std = sb("std", [BLOCK, SPAN])
        rstd = sb("rstd", [BLOCK, SPAN])
        fin = sb("fin", [BLOCK, BLOCKS, D])
        aggT = sb("aggT", [128, NODES])

        loads = sem("loads")
        xin_loaded = sem("xin_loaded")
        consts = sem("consts")
        vchain = sem("vchain")
        achain = sem("achain")
        wc_done = sem("wc_done")
        wc_ready = sem("wc_ready")
        params = sem("params")
        acc_zero = sem("acc_zero")
        z_done = sem("z_done")
        r_done = sem("r_done")
        y_done = sem("y_done")
        y_sb = sem("y_sb")
        var_done = sem("var_done")
        std_done = sem("std_done")
        x1_done = sem("x1_done")
        xt_done = sem("xt_done")
        x1T_done = sem("x1T_done")
        x1_stored = sem("x1_stored")
        agg_done = sem("agg_done")
        o_done = sem("o_done")
        fin_done = sem("fin_done")
        stored = sem("stored")
        L = [{n: sem(f"{n}{layer}") for n in ("idx", "ef", "gath", "e", "sum", "msg", "hot", "used", "turn")}
             for layer in range(2)]

        psZ = [[ps[:, (2 * h) * BANK:(2 * h) * BANK + LOW * BLOCK],
                ps[:, (2 * h + 1) * BANK:(2 * h + 1) * BANK + (SPAN - LOW) * BLOCK]] for h in range(HALVES)]
        psY = ps[0:BLOCK, 4 * BANK:4 * BANK + SPAN * D]
        psT = [ps[:, 6 * BANK:6 * BANK + LOW * BLOCK], ps[:, 7 * BANK:7 * BANK + (SPAN - LOW) * BLOCK]]
        psE = ps[:, 7 * BANK:8 * BANK]
        parts = [(0, LOW), (LOW, SPAN)]

        weights = [
            (we1T[:, :, :], We1T.rearrange("(h p) e -> p h e", p=128)),
            (we2[:, :, :], We2.rearrange("(h p) d -> p h d", p=128)),
            (be2_row[:, :], be2), (wm1[:, :], Wm1),
            (wm2[:, :, :], Wm2.rearrange("(h p) d -> p h d", p=128)),
            (w1T[:, :], W1T), (w2T[:, :], W2T),
            (eps1[:, :], eps.to_broadcast([128, 1])),
            (outb[:, 0, :], bb1.to_broadcast([128, D])), (outb[:, 1, :], bb2.to_broadcast([128, D])),
            (hT[:, :], xT), (dst_i[:, :], dst_t),
        ] + [(bn1[:, k, :], v) for k, v in enumerate((bm1, g1, b1, m1, v1))] \
          + [(bn2[:, k, :], v.to_broadcast([128, D])) for k, v in enumerate((bm2, g2, b2, m2, v2))]
        LOADED = 16 * len(weights)

        block = ctx.enter_context(nc.Block())

        def general_sp(sp, layer):
            s = L[layer]
            with sp.Fori(0, GROUPS) as g:
                sp.wait_ge(s["gath"], g * (16 * GROUP))
                sp.dma_start(idx[:, :], src_t[:, bass.ds(g * GROUP, GROUP)]).then_inc(s["idx"], 16)
                if layer == 0:
                    sp.wait_ge(s["e"], g)
                    sp.dma_start(ef[0:EF, :], efT[:, bass.ds(g * (GROUP * TILE), GROUP * TILE)]).then_inc(s["ef"], 16)

        def general_pool(pool, layer):
            s, table = L[layer], (x, x1_dram)[layer]
            with pool.Fori(0, GROUPS) as g:
                pool.wait_ge(s["idx"], g * 16 + 16)
                if layer == 0:
                    pool.wait_ge(s["sum"], g)
                else:
                    pool.wait_ge(s["used"], g * GROUP)
                pool.sem_inc(s["turn"], 1)
                for j in range(GROUP):
                    pool.indirect_dma_start(gath[:, j, :], None, table,
                                            bass.IndirectOffsetOnAxis(idx[:, j:j + 1], 0)).then_inc(s["gath"], 16)

        def general_pe(pe, layer):
            s = L[layer]
            rows = (msg, gath)[layer]
            pe.wait_ge(acc_zero, layer + 1)
            with pe.Fori(0, GROUPS) as g:
                if layer == 0:
                    pe.wait_ge(s["ef"], g * 16 + 16)
                    pe.wait_ge(s["sum"], g)
                    for j in range(GROUP):
                        mm = nc.tensor.matmul(psE[:, j * D:(j + 1) * D], ef[:, j * TILE:(j + 1) * TILE], wc[:, :],
                                              start=True, stop=True)
                    mm.then_inc(s["e"], 1)
                    pe.wait_ge(s["msg"], g + 1)
                else:
                    pe.wait_ge(s["gath"], g * (16 * GROUP) + 16 * GROUP)
                for j in range(GROUP):
                    pe.wait_ge(s["hot"], g * GROUP + (j + 1))
                    for c in range(0, NODES, BANK):
                        e = min(c + BANK, NODES)
                        mm = nc.tensor.matmul(ps[:, c:e], rows[:, j, :], hot[:, c:e], start=False, stop=True,
                                              skip_group_check=True)
                    mm.then_inc(s["used"], 1)

        def general_dve(dve, layer):
            s = L[layer]
            with dve.Fori(0, GROUPS) as g:
                if layer == 0:
                    dve.wait_ge(s["e"], g + 1)
                    dve.wait_ge(s["gath"], g * (16 * GROUP) + 16 * GROUP)
                    dve.wait_ge(s["msg"], g)
                    nc.vector.tensor_tensor(summed[:, :, :], psE.rearrange("p (j d) -> p j d", j=GROUP),
                                            gath[:, :, :], ALU.add).then_inc(s["sum"], 1)
                for j in range(GROUP):
                    dve.wait_ge(s["used"], g * GROUP + j)
                    nc.vector.tensor_scalar(hot[:, :], node_iota[:, :], dst_f[:, bass.ds(g * GROUP + j, 1)], None,
                                            ALU.is_equal).then_inc(s["hot"], 1)

        def general_act(act, layer):
            s = L[layer]
            if layer == 0:
                with act.Fori(0, GROUPS) as g:
                    act.wait_ge(s["sum"], g + 1)
                    act.wait_ge(s["used"], g * GROUP)
                    nc.scalar.activation(msg[:, :, :], summed[:, :, :], ACT.Relu).then_inc(s["msg"], 1)

        @block.sync
        def _(sp):
            sp.wait_ge(consts, 1)
            for dst, src in weights:
                sp.dma_start(dst, src).then_inc(loads, 16)
            sp.dma_start(x_in[:, :, :], x.rearrange("(b p) d -> p b d", p=BLOCK)).then_inc(xin_loaded, 16)
            general_sp(sp, 0)
            for b in range(SUPERS):
                sp.wait_ge(x1_done, b + 1)
                sp.dma_start(x1_dram[b * SNODES:(b + 1) * SNODES, :].rearrange("(k p) d -> p k d", p=BLOCK),
                             x1[:, b * SPAN:(b + 1) * SPAN, :]).then_inc(x1_stored, 16)
            general_sp(sp, 1)
            for b in range(SUPERS):
                sp.wait_ge(fin_done, b + 1)
                sp.dma_start(out[b * SNODES:(b + 1) * SNODES, :].rearrange("(k p) d -> p k d", p=BLOCK),
                             fin[:, b * SPAN:(b + 1) * SPAN, :]).then_inc(stored, 16)
            sp.wait_ge(stored, 16 * SUPERS)

        @block.gpsimd
        def _(pool):
            nc.gpsimd.memset(zeros[:, :], 0.0).then_inc(params, 1)
            nc.gpsimd.iota(node_iota[:, :], [[1, NODES]], base=0, channel_multiplier=0,
                           allow_small_or_imprecise_dtypes=True).then_inc(params, 1)
            pool.wait_ge(params, 2)
            nc.gpsimd.affine_select(out=ident[:, :], in_=zeros[:, :], compare_op=ALU.not_equal, fill=1.0, base=0,
                                    pattern=[[-1, 128]], channel_multiplier=1).then_inc(params, 1)
            general_pool(pool, 0)
            pool.wait_ge(x1_stored, 16 * SUPERS)
            general_pool(pool, 1)

        @block.scalar
        def _(act):
            act.wait_ge(vchain, 2)
            nc.scalar.activation(tmp1[:, 1, :], tmp1[:, 0, :], ACT.Sqrt).then_inc(achain, 1)
            nc.scalar.activation(tmp2[:, 1, :], tmp2[:, 0, :], ACT.Sqrt).then_inc(achain, 1)
            general_act(act, 0)
            act.wait_ge(params, 4)
            for b in range(SUPERS):
                act.wait_ge(z_done, b + 1)
                if b:
                    act.wait_ge(y_done, b)
                for h in range(HALVES):
                    for lo, hi in parts:
                        last = nc.scalar.activation(rT[:, h, lo * BLOCK:hi * BLOCK], psZ[h][lo > 0], ACT.Relu,
                                                    bias=bias1[:, h:h + 1], scale=scale1[:, h:h + 1])
                last.then_inc(r_done, 1)
                act.wait_ge(var_done, b + 1)
                nc.scalar.activation(std[:, :], mv[:, :, 1], ACT.Sqrt, bias=epsc[0:BLOCK, 1:2]).then_inc(std_done, 1)
                act.wait_ge(xt_done, b + 1)
                for lo, hi in parts:
                    last = nc.scalar.copy(x1T[:, b * SNODES + lo * BLOCK:b * SNODES + hi * BLOCK], psT[lo > 0])
                last.then_inc(x1T_done, 1)
            for b in range(SUPERS):
                act.wait_ge(var_done, SUPERS + b + 1)
                nc.scalar.activation(std[:, :], mv[:, :, 1], ACT.Sqrt, bias=epsc[0:BLOCK, 1:2]).then_inc(std_done, 1)

        def norm(dve, link, b, n, to, done):
            for k in range(SPAN):
                last = nc.vector.bn_stats(stats[:, k, :], y[:, k, :])
            link(last)
            if n:
                dve.wait_ge(std_done, n)
            for k in range(SPAN):
                last = nc.vector.bn_aggr(mv[:, k, :], stats[:, k, :])
            last.then_inc(var_done, 1)
            dve.wait_ge(std_done, n + 1)
            link(nc.vector.reciprocal(rstd[:, :], std[:, :]))
            for k in range(SPAN):
                last = nc.vector.tensor_scalar(to[:, k, :], y[:, k, :], mv[:, k, 0:1], rstd[:, k:k + 1],
                                               ALU.subtract, ALU.mult)
            last.then_inc(done, 1)

        @block.vector
        def _(dve):
            count = [0]

            def link(ins):
                count[0] += 1
                ins.then_inc(vchain, 1)
                dve.wait_ge(vchain, count[0])

            nc.vector.memset(ef[:, :], 1.0)
            nc.vector.memset(unit_row[:, 0:EF], 0.0)
            nc.vector.memset(unit_row[:, EF:EF + 1], 1.0)
            nc.vector.memset(epsc[:, 1:2], LN_EPS)
            nc.vector.memset(ps[:, :], 0.0).then_inc(acc_zero, 1)
            dve.wait_ge(acc_zero, 1)
            nc.vector.memset(epsc[:, 0:1], BN_EPS).then_inc(consts, 1)
            dve.wait_ge(loads, LOADED)
            link(nc.vector.tensor_scalar(tmp1[:, 0, :], bn1[:, 4, :], BN_EPS, None, ALU.add))
            link(nc.vector.tensor_scalar(tmp2[:, 0, :], bn2[:, 4, :], BN_EPS, None, ALU.add))
            dve.wait_ge(achain, 2)
            link(nc.vector.reciprocal(tmp1[:, 2, :], tmp1[:, 1, :]))
            link(nc.vector.reciprocal(tmp2[:, 2, :], tmp2[:, 1, :]))
            link(nc.vector.tensor_tensor(scale1[:, :], tmp1[:, 2, :], bn1[:, 1, :], ALU.mult))
            link(nc.vector.tensor_tensor(scale2[:, :], tmp2[:, 2, :], bn2[:, 1, :], ALU.mult))
            link(nc.vector.tensor_tensor(tmp1[:, 3, :], bn1[:, 0, :], bn1[:, 3, :], ALU.subtract))
            link(nc.vector.tensor_tensor(tmp2[:, 3, :], bn2[:, 0, :], bn2[:, 3, :], ALU.subtract))
            link(nc.vector.tensor_tensor(tmp1[:, 0, :], tmp1[:, 3, :], scale1[:, :], ALU.mult))
            link(nc.vector.tensor_tensor(tmp2[:, 0, :], tmp2[:, 3, :], scale2[:, :], ALU.mult))
            link(nc.vector.tensor_tensor(bias1[:, :], tmp1[:, 0, :], bn1[:, 2, :], ALU.add))
            link(nc.vector.tensor_tensor(bias2[:, :], tmp2[:, 0, :], bn2[:, 2, :], ALU.add))
            link(nc.vector.tensor_tensor(biasO[:, :], outb[:, 0, :], outb[:, 1, :], ALU.add))
            link(nc.vector.tensor_scalar(eps1p[:, :], eps1[:, :], 1.0, None, ALU.add))
            for h in range(HALVES):
                link(nc.vector.tensor_tensor(wm2[:, h, :], wm2[:, h, :], scale2[:, :], ALU.mult))
            link(nc.vector.tensor_scalar(hT[:, :], hT[:, :], eps1p[:, 0:1], None, ALU.mult))
            dve.wait_ge(xin_loaded, 16)
            for b in range(BLOCKS):
                last = nc.vector.tensor_tensor(x_in[:, b, :], x_in[:, b, :], bias2[0:BLOCK, :], ALU.add)
            link(last)
            dve.wait_ge(wc_done, 1)
            nc.vector.tensor_copy(wc[:, :], psE[0:EF + 1, 0:D]).then_inc(wc_ready, 1)
            dve.wait_ge(params, 3)
            link(nc.vector.tensor_copy(dst_f[:, :], dst_i[:, :]))
            general_dve(dve, 0)
            dve.wait_ge(L[0]["used"], TILES)
            link(nc.vector.tensor_tensor(hT[:, :], hT[:, :], ps[:, 0:NODES], ALU.add))
            nc.vector.memset(zeros[:, 0:1], 0.0).then_inc(params, 1)
            for b in range(SUPERS):
                dve.wait_ge(y_done, b + 1)
                if b:
                    dve.wait_ge(x1_done, b)
                for lo, hi in parts:
                    last = nc.vector.tensor_tensor(
                        y[:, lo:hi, :], psY[:, lo * D:hi * D].rearrange("p (k d) -> p k d", d=D),
                        x_in[:, b * SPAN + lo:b * SPAN + hi, :], ALU.add)
                last.then_inc(y_sb, 1)
                dve.wait_ge(y_sb, b + 1)
                norm(dve, link, b, b, x1[:, b * SPAN:(b + 1) * SPAN, :], x1_done)
            dve.wait_ge(x1T_done, SUPERS)
            nc.vector.memset(ps[:, :], 0.0).then_inc(acc_zero, 1)
            general_dve(dve, 1)
            dve.wait_ge(L[1]["used"], TILES)
            nc.vector.tensor_copy(aggT[:, :], ps[:, 0:NODES]).then_inc(agg_done, 1)
            for b in range(BLOCKS):
                last = nc.vector.tensor_tensor(x1[:, b, :], x1[:, b, :], biasO[0:BLOCK, :], ALU.add)
            link(last)
            for b in range(SUPERS):
                dve.wait_ge(o_done, b + 1)
                if b:
                    dve.wait_ge(fin_done, b)
                for lo, hi in parts:
                    last = nc.vector.tensor_tensor(
                        y[:, lo:hi, :], psY[:, lo * D:hi * D].rearrange("p (k d) -> p k d", d=D),
                        x1[:, b * SPAN + lo:b * SPAN + hi, :], ALU.add)
                last.then_inc(y_sb, 1)
                dve.wait_ge(y_sb, SUPERS + b + 1)
                norm(dve, link, b, SUPERS + b, fin[:, b * SPAN:(b + 1) * SPAN, :], fin_done)

        @block.tensor
        def _(pe):
            pe.wait_ge(loads, LOADED)
            pe.wait_ge(consts, 1)
            for h in range(HALVES):
                nc.tensor.matmul(psE[0:EF + 1, 0:D], we1T[:, h, :], we2[:, h, :], start=(h == 0), stop=False)
            nc.tensor.matmul(psE[0:EF + 1, 0:D], unit_row[:, :], be2_row[:, :], start=False, stop=True)\
                .then_inc(wc_done, 1)
            pe.wait_ge(wc_ready, 1)
            general_pe(pe, 0)
            pe.wait_ge(params, 4)
            for b in range(SUPERS):
                if b:
                    pe.wait_ge(r_done, b)
                for h in range(HALVES):
                    for lo, hi in parts:
                        last = nc.tensor.matmul(psZ[h][lo > 0], wm1[:, h * 128:(h + 1) * 128],
                                                hT[:, b * SNODES + lo * BLOCK:b * SNODES + hi * BLOCK],
                                                start=True, stop=True)
                last.then_inc(z_done, 1)
                pe.wait_ge(r_done, b + 1)
                if b:
                    pe.wait_ge(y_sb, b)
                for k in range(SPAN):
                    for h in range(HALVES):
                        last = nc.tensor.matmul(psY[:, k * D:(k + 1) * D], rT[:, h, k * BLOCK:(k + 1) * BLOCK],
                                                wm2[:, h, :], start=(h == 0), stop=(h == HALVES - 1))
                last.then_inc(y_done, 1)
                pe.wait_ge(x1_done, b + 1)
                if b:
                    pe.wait_ge(x1T_done, b)
                for k in range(SPAN):
                    p, at = int(k >= LOW), (k - LOW * (k >= LOW)) * BLOCK
                    last = nc.tensor.transpose(psT[p][:, at:at + BLOCK], x1[:, b * SPAN + k, :],
                                               ident[0:BLOCK, 0:BLOCK])
                last.then_inc(xt_done, 1)
            pe.wait_ge(x1T_done, SUPERS)
            general_pe(pe, 1)
            pe.wait_ge(agg_done, 1)
            for b in range(SUPERS):
                if b:
                    pe.wait_ge(y_sb, SUPERS + b)
                for k in range(SPAN):
                    n = b * SNODES + k * BLOCK
                    for i, (rows, w) in enumerate(((x1T, w1T), (aggT, w2T))):
                        last = nc.tensor.matmul(psY[:, k * D:(k + 1) * D], rows[:, n:n + BLOCK], w[:, :],
                                                start=(i == 0), stop=(i == 1))
                last.then_inc(o_done, 1)


def kernel(x, src, dst, edge_attr_16, L0_gnn_We1, L0_gnn_be1, L0_gnn_We2, L0_gnn_be2, L0_gnn_eps, L0_gnn_Wm1,
           L0_gnn_bm1, L0_gnn_g1, L0_gnn_b1, L0_gnn_m1, L0_gnn_v1, L0_gnn_Wm2, L0_gnn_bm2, L0_gnn_g2, L0_gnn_b2,
           L0_gnn_m2, L0_gnn_v2, L1_gnn_W1, L1_gnn_b1, L1_gnn_W2, L1_gnn_b2):
    import numpy as np
    import concourse.bacc as bacc
    from concourse.bass_utils import run_bass_kernel_spmd

    def per_edge(a, fill):
        flat = np.concatenate([np.asarray(a), np.full(TILES * TILE - EDGES, fill, np.asarray(a).dtype)])
        return np.ascontiguousarray(flat.reshape(TILES, TILE).T)

    def halves(a):
        return np.ascontiguousarray(np.asarray(a).reshape(HALVES, 128).T)

    def row(a):
        return np.asarray(a).reshape(1, -1)

    ef = np.asarray(edge_attr_16)
    ef = np.concatenate([ef, np.zeros((TILES * TILE - EDGES, EF), ef.dtype)])
    data = {
        "x": np.asarray(x), "xT": np.ascontiguousarray(np.asarray(x).T),
        "src_t": per_edge(src, 0), "dst_t": per_edge(dst, NODES),
        "efT": np.ascontiguousarray(ef.T), "We1T": np.ascontiguousarray(np.concatenate([np.asarray(L0_gnn_We1), row(L0_gnn_be1)]).T),
        "We2": np.asarray(L0_gnn_We2), "be2": row(L0_gnn_be2), "eps": row(L0_gnn_eps),
        "Wm1": np.asarray(L0_gnn_Wm1), "bm1": halves(L0_gnn_bm1), "g1": halves(L0_gnn_g1), "b1": halves(L0_gnn_b1),
        "m1": halves(L0_gnn_m1), "v1": halves(L0_gnn_v1), "Wm2": np.asarray(L0_gnn_Wm2), "bm2": row(L0_gnn_bm2),
        "g2": row(L0_gnn_g2), "b2": row(L0_gnn_b2), "m2": row(L0_gnn_m2), "v2": row(L0_gnn_v2),
        "W1T": np.ascontiguousarray(np.asarray(L1_gnn_W1).T), "bb1": row(L1_gnn_b1),
        "W2T": np.ascontiguousarray(np.asarray(L1_gnn_W2).T), "bb2": row(L1_gnn_b2),
    }
    nc = bacc.Bacc("TRN2", target_bir_lowering=False, num_devices=1)
    arrays, args = {}, []
    for name, a in data.items():
        arrays[f"in_{name}"] = a
        args.append(nc.dram_tensor(f"in_{name}", a.shape, mybir.dt.from_np(a.dtype), kind="ExternalInput").ap())
    args.append(nc.dram_tensor("out_0", (NODES, D), F32, kind="ExternalOutput").ap())
    args.append(nc.dram_tensor("x1_rows", (NODES, D), F32, kind="Internal").ap())
    gnn_kernel(nc, *args)
    result = run_bass_kernel_spmd(nc, [arrays], core_ids=[0])
    return result.results[0]["out_0"]
```

```python
from contextlib import ExitStack

import concourse.bass as bass
from concourse import mybir

F32 = mybir.dt.float32
I32 = mybir.dt.int32
F16 = mybir.dt.float16
BF16 = mybir.dt.bfloat16
ALU = mybir.AluOpType
ACT = mybir.ActivationFunctionType
AX_X = mybir.AxisListType.X

NODES, D, HID, EF = 3125, 128, 256, 16
EDGES = 53125
P = 128
GROUP = 4
GEDGES = GROUP * P
GROUPS = -(-EDGES // GEDGES)
TILES = GROUPS * GROUP
BLOCK = 128
BLOCKS = -(-NODES // BLOCK)
ROWS = BLOCKS * BLOCK
SPAN = 5
SUPERS = BLOCKS // SPAN
SNODES = SPAN * BLOCK
LOW = 3
BANK = 512
HALVES = HID // P
WIN = 39
LOWB = BANK // WIN
WCOLS = BLOCKS * WIN
UNROLL = 4
PARTS = 3
BN_EPS, LN_EPS = 0.001, 1e-05


def gnn_kernel(nc, x, xT, src_t, dst_t, dst_a, dst_b, first, last, third, efT, We1T, We2, be2, eps, Wm1,
               bm1, g1, b1, m1, v1, Wm2, bm2, g2, b2, m2, v2, W1T, bb1, W2T, bb2, out, x1_dram):
    with ExitStack() as ctx:
        def sb(name, shape, dt=F32):
            return ctx.enter_context(nc.sbuf_tensor(name, shape, dt))

        def sem(name):
            return ctx.enter_context(nc.semaphore(name))

        ps = ctx.enter_context(nc.psum_tensor("ps", [P, 8 * BANK], F32))

        AT = sb("AT", [P, BLOCKS, NODES + WIN], F16)
        hT = sb("hT", [P, ROWS + WIN + 1])
        x1T = hT
        work = sb("work", [P, 8000])

        class Carver:
            def __init__(self, ap, words):
                self.ap, self.at, self.words = ap, 0, words

            def take(self, words, dt=F32):
                a = self.ap[:, self.at:self.at + words]
                self.at += words
                assert self.at <= self.words
                return a if dt == F32 else a.bitcast(dt)

        edge = Carver(work, 8000)
        gath = edge.take(UNROLL * GROUP * D).rearrange("p (g j d) -> p g j d", g=UNROLL, j=GROUP)
        ef = edge.take(2 * GEDGES).rearrange("p (g e) -> p g e", g=2)
        mv = edge.take(GROUP * (WCOLS + 1) // 2, F16).rearrange("p (j c) -> p j c", j=GROUP)
        ob = edge.take(2 * (GROUP - 1) * 64, F16).rearrange("p (g j b) -> p g j b", g=2, j=GROUP - 1)
        ob_last = edge.take(UNROLL * 64, F16).rearrange("p (g b) -> p g b", g=UNROLL)
        od = edge.take(2 * GROUP * WIN).rearrange("p (g j w) -> p g j w", g=2, j=GROUP)
        mvc = edge.take(BLOCKS + 1, F16)[:, 0:2 * BLOCKS].rearrange("p (g a) -> p g a", g=2)
        b_key = edge.take(TILES)
        m_key = edge.take(TILES)
        d_key = edge.take(TILES)
        c_key = edge.take(GROUPS)
        iota = edge.take((WCOLS + 1) // 2, F16)

        node = Carver(work, 8000)
        x1p = node.take(PARTS * BLOCKS * D // 2, BF16).rearrange("p (k b d) -> p k b d", k=PARTS, b=BLOCKS)
        x_in = node.take(SPAN * D).rearrange("p (k d) -> p k d", k=SPAN)
        y = node.take(SPAN * D).rearrange("p (k d) -> p k d", k=SPAN)
        x1s = node.take(SPAN * D).rearrange("p (k d) -> p k d", k=SPAN)
        rT_f = node.take(HALVES * SNODES)
        rT = rT_f.rearrange("p (h n) -> p h n", h=HALVES)
        aggT = rT_f[:, 0:2 * BANK].rearrange("p (g n) -> p g n", g=2)

        AT_w = AT[:, :, :].rearrange("p a n -> p (a n)")[:, 0:2 * 12000].bitcast(F32)
        early = Carver(AT_w, 12000)
        src_i = early.take(TILES, I32)
        dst_i = early.take(TILES, I32)
        dst_ai = early.take(TILES, I32)
        dst_bi = early.take(TILES, I32)
        t_i = early.take(TILES, I32)
        a_f = early.take(TILES)
        t_f = early.take(TILES)
        base_b = early.take(GROUPS, I32)
        last_i = early.take(GROUPS, I32)
        third_i = early.take(GROUPS, I32)
        t_g = early.take(GROUPS)
        we1T = early.take(HALVES * (EF + 1)).rearrange("p (h e) -> p h e", h=HALVES)
        we2 = early.take(HALVES * D).rearrange("p (h d) -> p h d", h=HALVES)
        bn2 = early.take(5 * D).rearrange("p (k d) -> p k d", k=5)
        tmp2 = early.take(4 * D).rearrange("p (k d) -> p k d", k=4)
        outb = early.take(2 * D).rearrange("p (k d) -> p k d", k=2)
        be2_row = early.take(D)[0:1, :]
        unit_row = early.take(EF + 1)[0:1, :]
        general = Carver(AT_w, 12000)
        general.take(early.at)
        hot = general.take(NODES)
        dst_f = general.take(TILES)
        node_iota = general.take(NODES)

        wc = sb("wc", [EF + 1, D])
        wm1 = sb("wm1", [P, HID])
        wm2 = sb("wm2", [P, HALVES, D])
        w1T = sb("w1T", [P, D])
        w2T = sb("w2T", [P, D])
        bn1 = sb("bn1", [P, 5, HALVES])
        tmp1 = sb("tmp1", [P, 4, HALVES])
        scale1 = sb("scale1", [P, HALVES])
        bias1 = sb("bias1", [P, HALVES])
        scale2 = sb("scale2", [P, D])
        bias2 = sb("bias2", [P, D])
        biasO = sb("biasO", [P, D])
        eps1 = sb("eps1", [P, 1])
        eps1p = sb("eps1p", [P, 1])
        epsc = sb("epsc", [P, 1])
        ones = sb("ones", [P, 1])
        viol = sb("viol", [P, 4])
        flag = sb("flag", [1, 1], I32)
        bases = sb("bases", [1, GROUPS], I32)
        ident = sb("ident", [P, P])
        stats = sb("stats", [P, SPAN, 6])
        mean_var = sb("mean_var", [P, SPAN, 2])
        std = sb("std", [P, SPAN])
        rstd = sb("rstd", [P, SPAN])

        keys_loaded = sem("keys_loaded")
        loads = sem("loads")
        pool_consts = sem("pool_consts")
        consts = sem("consts")
        vchain = sem("vchain")
        achain = sem("achain")
        viol_done = sem("viol_done")
        viol_sum = sem("viol_sum")
        flag_done = sem("flag_done")
        keys_done = sem("keys_done")
        wc_done = sem("wc_done")
        wc_ready = sem("wc_ready")
        sums_done = sem("sums_done")
        x_loaded = sem("x_loaded")
        z_done = sem("z_done")
        r_done = sem("r_done")
        y_done = sem("y_done")
        y_sb = sem("y_sb")
        var_done = sem("var_done")
        std_done = sem("std_done")
        x1_done = sem("x1_done")
        xt_done = sem("xt_done")
        x1T_done = sem("x1T_done")
        hi_done = sem("hi_done")
        rest_done = sem("rest_done")
        mid_done = sem("mid_done")
        lo_done = sem("lo_done")
        x1_stored = sem("x1_stored")
        x1_back = [sem(f"x1_back{k}") for k in range(2)]
        res_done = sem("res_done")
        acc_done = sem("acc_done")
        agg_done = sem("agg_done")
        o_done = sem("o_done")
        fin_done = sem("fin_done")
        stored = sem("stored")
        ef_in = [sem(f"ef_in{k}") for k in range(2)]
        idx_in = [sem(f"idx_in{k}") for k in range(UNROLL)]
        gathered = [sem(f"gathered{k}") for k in range(UNROLL)]
        turn = sem("turn")
        e_done = sem("e_done")
        sum_done = sem("sum_done")
        msg_done = sem("msg_done")
        od_done = sem("od_done")
        p_done = sem("p_done")
        added = sem("added")
        ob_done = sem("ob_done")
        mv_done = sem("mv_done")
        mv_used = sem("mv_used")
        mvc_done = sem("mvc_done")
        a_done = sem("a_done")
        copied = sem("copied")
        acc_zero = sem("acc_zero")
        G = [{n: sem(f"g{n}{layer}") for n in ("idx", "ef", "gath", "e", "sum", "msg", "hot", "used", "turn")}
             for layer in range(2)]

        idx = sb("idx", [P, UNROLL, GROUP], I32)

        psE = [ps[:, k * BANK:(k + 1) * BANK] for k in range(2)]
        psP = [ps[:, (2 + k) * BANK:(2 + k) * BANK + WIN] for k in range(2)]
        psA = [[ps[:, (4 + 2 * k + i) * BANK:(4 + 2 * k + i) * BANK + n * WIN] for i, n in
                enumerate((LOWB, BLOCKS - LOWB))] for k in range(2)]
        gE = ps[:, 7 * BANK:8 * BANK]
        psZ = [[ps[:, (2 * h) * BANK:(2 * h) * BANK + LOW * BLOCK],
                ps[:, (2 * h + 1) * BANK:(2 * h + 1) * BANK + (SPAN - LOW) * BLOCK]] for h in range(HALVES)]
        psY = ps[:, 4 * BANK:4 * BANK + SNODES]
        psT = [ps[:, 6 * BANK:6 * BANK + LOW * BLOCK], ps[:, 7 * BANK:7 * BANK + (SPAN - LOW) * BLOCK]]
        parts = [(0, LOW), (LOW, SPAN)]
        windows = [(0, LOWB), (LOWB, BLOCKS)]
        chunks = [(n, min(n + BANK, NODES)) for n in range(0, NODES, BANK)]

        key_loads = [
            (dst_ai, dst_a), (dst_bi, dst_b), (base_b, first.to_broadcast([P, GROUPS])), (last_i[0:1, :], last),
            (third_i[0:1, :], third), (bases[:, :], first), (src_i, src_t), (dst_i, dst_t),
        ]
        weights = [
            (we1T, We1T.rearrange("(h p) e -> p h e", p=P)),
            (we2, We2.rearrange("(h p) d -> p h d", p=P)),
            (be2_row, be2), (bn1[:, :, :], None), (eps1[:, :], eps.to_broadcast([P, 1])),
            (hT[:, 0:ROWS], xT), (wm1[:, :], Wm1),
            (wm2[:, :, :], Wm2.rearrange("(h p) d -> p h d", p=P)),
            (w1T[:, :], W1T), (w2T[:, :], W2T),
            (outb[:, 0, :], bb1.to_broadcast([P, D])), (outb[:, 1, :], bb2.to_broadcast([P, D])),
        ]
        weights = [w for w in weights if w[1] is not None] \
            + [(bn1[:, k, :], v) for k, v in enumerate((bm1, g1, b1, m1, v1))] \
            + [(bn2[:, k, :], v.to_broadcast([P, D])) for k, v in enumerate((bm2, g2, b2, m2, v2))]

        block = ctx.enter_context(nc.Block())

        def general_sp(sp, layer):
            s = G[layer]
            with sp.Fori(0, GROUPS) as g:
                sp.wait_ge(s["turn"], g + 1)
                sp.dma_start(idx[:, 0, :], src_t[:, bass.ds(g * GROUP, GROUP)]).then_inc(s["idx"], 16)
                if layer == 0:
                    sp.dma_start(ef[0:EF, 0, :], efT[:, bass.ds(g * GEDGES, GEDGES)]).then_inc(s["ef"], 16)

        def general_pool(pool, layer):
            s, table = G[layer], (x, x1_dram)[layer]
            with pool.Fori(0, GROUPS) as g:
                pool.wait_ge(s["idx"], g * 16 + 16)
                pool.sem_inc(turn, 1)
                for j in range(GROUP):
                    pool.indirect_dma_start(gath[:, 0, j, :], None, table,
                                            bass.IndirectOffsetOnAxis(idx[:, 0, j:j + 1], 0)).then_inc(s["gath"], 16)

        def general_pe(pe, layer):
            s = G[layer]
            pe.wait_ge(acc_zero, layer + 1)
            pe.sem_inc(s["turn"], 1)
            with pe.Fori(0, GROUPS) as g:
                if layer == 0:
                    pe.wait_ge(s["ef"], g * 16 + 16)
                    for j in range(GROUP):
                        mm = nc.tensor.matmul(gE[:, j * D:(j + 1) * D], ef[0:EF + 1, 0, j * P:(j + 1) * P],
                                              wc[:, :], start=True, stop=True)
                    mm.then_inc(s["e"], 1)
                    pe.wait_ge(s["msg"], g + 1)
                else:
                    pe.wait_ge(s["gath"], g * (16 * GROUP) + 16 * GROUP)
                for j in range(GROUP):
                    pe.wait_ge(s["hot"], g * GROUP + (j + 1))
                    for c, e in chunks:
                        mm = nc.tensor.matmul(ps[:, c:e], gath[:, 0, j, :], hot[:, c:e], start=False, stop=True,
                                              skip_group_check=True)
                    mm.then_inc(s["used"], 1)
                nc.tensor.matmul(gE[0:1, 0:1], ones[:, :], ones[:, :], start=True, stop=True).then_inc(s["turn"], 1)

        def general_dve(dve, layer):
            s = G[layer]
            nc.vector.memset(ps[:, :], 0.0).then_inc(acc_zero, 1)
            dve.sem_inc(s["used"], 1)
            with dve.Fori(0, GROUPS) as g:
                if layer == 0:
                    dve.wait_ge(s["e"], g + 1)
                    dve.wait_ge(s["gath"], g * (16 * GROUP) + 16 * GROUP)
                    nc.vector.tensor_tensor(gath[:, 0, :, :], gE.rearrange("p (j d) -> p j d", j=GROUP),
                                            gath[:, 0, :, :], ALU.add).then_inc(s["sum"], 1)
                for j in range(GROUP):
                    dve.wait_ge(s["used"], g * GROUP + (j + 1))
                    nc.vector.tensor_scalar(hot, node_iota, dst_f[:, bass.ds(g * GROUP + j, 1)], None,
                                            ALU.is_equal).then_inc(s["hot"], 1)
            dve.wait_ge(s["used"], TILES + 1)

        def general_act(act):
            s = G[0]
            with act.Fori(0, GROUPS) as g:
                act.wait_ge(s["sum"], g + 1)
                nc.scalar.activation(gath[:, 0, :, :], gath[:, 0, :, :], ACT.Relu).then_inc(s["msg"], 1)

        TURNS = GROUPS // UNROLL

        def edges_sp(sp):
            def load_ef(i, u):
                sp.dma_start(ef[0:EF, u % 2, :], efT[:, bass.ds(i * (UNROLL * GEDGES) + u * GEDGES, GEDGES)])\
                    .then_inc(ef_in[u % 2], 16)

            def turn_of(i, last_turn):
                for u in range(UNROLL):
                    g = i * UNROLL + u
                    sp.wait_ge(sum_done, g + 1)
                    sp.dma_start(idx[:, u, :], src_t[:, bass.ds(i * (UNROLL * GROUP) + u * GROUP, GROUP)])\
                        .then_inc(idx_in[u], 16)
                    if not (last_turn and u == UNROLL - 1):
                        sp.wait_ge(e_done, g + 2)
                        load_ef(i, u + 1)

            load_ef(0, 0)
            with sp.Fori(0, TURNS - 1) as i:
                turn_of(i, False)
            turn_of(TURNS - 1, True)

        def edges_pool(pool):
            with pool.Fori(0, TURNS) as i:
                for u in range(UNROLL):
                    g = i * UNROLL + u
                    pool.wait_ge(idx_in[u], i * 16 + 16)
                    pool.wait_ge(p_done, g + 1)
                    pool.sem_inc(turn, 1)
                    for j in range(GROUP):
                        pool.indirect_dma_start(gath[:, u, j, :], None, x,
                                                bass.IndirectOffsetOnAxis(idx[:, u, j:j + 1], 0))\
                            .then_inc(gathered[u], 16)

        def edges_pe(pe):
            def features(i, u):
                g, k = i * UNROLL + u, u % 2
                pe.wait_ge(ef_in[k], i * (16 * UNROLL // 2) + (16 * (u // 2) + 16))
                pe.wait_ge(sum_done, g + 3)
                for j in range(GROUP):
                    mm = nc.tensor.matmul(psE[k][:, j * D:(j + 1) * D], ef[0:EF + 1, k, j * P:(j + 1) * P],
                                          wc[:, :], start=True, stop=True)
                mm.then_inc(e_done, 1)

            def sums(i, u):
                g, k = i * UNROLL + u, u % 2
                pe.wait_ge(od_done, g + 1)
                pe.wait_ge(added, g + 1)
                pe.wait_ge(msg_done, g + 1)
                for j in range(GROUP):
                    mm = nc.tensor.matmul(psP[k], gath[:, u % UNROLL, j, :], od[:, k, j, :],
                                          start=(j == 0), stop=(j == GROUP - 1))
                mm.then_inc(p_done, 1)

            def counts(i, u):
                g, k, slot = i * UNROLL + u, u % 2, u % UNROLL
                pe.wait_ge(copied, g + 1)
                pe.wait_ge(ob_done, g + 1)
                for j in range(GROUP):
                    pe.wait_ge(mv_done, i * (UNROLL * GROUP) + (u * GROUP + j + 1))
                    own = ob[:, k, j, :] if j < GROUP - 1 else ob_last[:, slot, :]
                    for w, (a0, a1) in enumerate(windows):
                        mm = nc.tensor.matmul(psA[k][w], own, mv[:, j, a0 * WIN:a1 * WIN],
                                              start=(j == 0), stop=False, skip_group_check=True)
                    mm.then_inc(mv_used, 1)
                pe.wait_ge(mvc_done, g + 1)
                for w, (a0, a1) in enumerate(windows):
                    mm = nc.tensor.matmul(psA[k][w].rearrange("p (a w) -> p a w", w=WIN)[:, :, 0],
                                          ob_last[:, (slot - 1) % UNROLL, :], mvc[:, k, a0:a1],
                                          start=False, stop=True, skip_group_check=True)
                mm.then_inc(a_done, 1)

            def turn_of(i, last_turn):
                for u in range(UNROLL):
                    more = not (last_turn and u == UNROLL - 1)
                    if more:
                        features(i, u + 1)
                    sums(i, u)
                    if more:
                        counts(i, u + 1)

            features(0, 0)
            counts(0, 0)
            with pe.Fori(0, TURNS - 1) as i:
                turn_of(i, False)
            turn_of(TURNS - 1, True)

        def edges_dve(dve):
            def one_hots(i, u):
                g, k, slot = i * UNROLL + u, u % 2, u % UNROLL
                t = i * (UNROLL * GROUP) + u * GROUP
                dve.wait_ge(a_done, g + 1)
                for j in range(GROUP):
                    own = ob[:, k, j, :] if j < GROUP - 1 else ob_last[:, slot, :]
                    ins = nc.vector.tensor_scalar(own, iota[:, 0:BLOCK], b_key[:, bass.ds(t + j, 1)], None,
                                                  ALU.is_equal)
                ins.then_inc(ob_done, 1)
                for j in range(GROUP):
                    dve.wait_ge(mv_used, t + (j + 1))
                    nc.vector.tensor_scalar(mv[:, j, 0:WCOLS], iota[:, 0:WCOLS], m_key[:, bass.ds(t + j, 1)],
                                            None, ALU.is_equal).then_inc(mv_done, 1)
                nc.vector.tensor_scalar(mvc[:, k, :], iota[:, 0:BLOCKS], c_key[:, bass.ds(g, 1)], None,
                                        ALU.is_equal).then_inc(mvc_done, 1)
                dve.wait_ge(p_done, g + 3)
                nc.vector.tensor_tensor(od[:, k, :, :],
                                        iota[:, 0:WIN].unsqueeze(1).to_broadcast([P, GROUP, WIN]),
                                        d_key[:, bass.ds(t, GROUP)].unsqueeze(2).to_broadcast([P, GROUP, WIN]),
                                        ALU.is_equal).then_inc(od_done, 1)

            def turn_of(i, last_turn):
                for u in range(UNROLL):
                    g, k = i * UNROLL + u, u % 2
                    dve.wait_ge(e_done, g + 3)
                    dve.wait_ge(gathered[u], i * (16 * GROUP) + 16 * GROUP)
                    nc.vector.tensor_tensor(gath[:, u, :, :], psE[k].rearrange("p (j d) -> p j d", j=GROUP),
                                            gath[:, u, :, :], ALU.add).then_inc(sum_done, 1)
                    if not (last_turn and u == UNROLL - 1):
                        one_hots(i, u + 1)
                    base = dve.value_load(bases[0:1, bass.ds(g, 1)], min_val=0, max_val=NODES - 1)
                    dve.wait_ge(p_done, g + 5)
                    to = hT[:, bass.ds(base, WIN)]
                    nc.vector.tensor_tensor(to, psP[k], to, ALU.add).then_inc(added, 1)

            one_hots(0, 0)
            with dve.Fori(0, TURNS - 1) as i:
                turn_of(i, False)
            turn_of(TURNS - 1, True)

        def edges_act(act):
            def copy_counts(i, u):
                g, k = i * UNROLL + u, u % 2
                base = act.value_load(bases[0:1, bass.ds(g, 1)], min_val=0, max_val=NODES - 1)
                act.wait_ge(a_done, g + 3)
                for w, (a0, a1) in enumerate(windows):
                    ins = nc.scalar.copy(AT[:, a0:a1, bass.ds(base, WIN)],
                                         psA[k][w].rearrange("p (a w) -> p a w", w=WIN))
                ins.then_inc(copied, 1)

            def turn_of(i, last_turn):
                for u in range(UNROLL):
                    act.wait_ge(sum_done, i * UNROLL + (u + 5))
                    nc.scalar.activation(gath[:, u, :, :], gath[:, u, :, :], ACT.Relu).then_inc(msg_done, 1)
                    if not (last_turn and u == UNROLL - 1):
                        copy_counts(i, u + 1)

            copy_counts(0, 0)
            with act.Fori(0, TURNS - 1) as i:
                turn_of(i, False)
            turn_of(TURNS - 1, True)

        def aggregate_pe(pe):
            def finish(c):
                n0, n1 = chunks[c]
                pe.wait_ge(agg_done, c + 1)
                if c >= 2:
                    pe.wait_ge(y_sb, SUPERS + c - 1)
                for b, n in enumerate(range(n0, n1, BLOCK)):
                    m = min(BLOCK, n1 - n)
                    for i, (rows, w) in enumerate(((x1T[:, n:n + m], w1T),
                                                   (aggT[:, c % 2, b * BLOCK:b * BLOCK + m], w2T))):
                        mm = nc.tensor.matmul(ps[0:m, (2 + c % 2) * BANK + b * D:(2 + c % 2) * BANK + (b + 1) * D],
                                              rows, w[:, :], start=(i == 0), stop=(i == 1))
                mm.then_inc(o_done, 1)

            for c, (n0, n1) in enumerate(chunks):
                if c >= 2:
                    pe.wait_ge(agg_done, c - 1)
                if c == 0:
                    pe.wait_ge(lo_done, SUPERS)
                for b in range(BLOCKS):
                    for q in range(PARTS):
                        mm = nc.tensor.matmul(ps[:, (c % 2) * BANK:(c % 2) * BANK + n1 - n0], x1p[:, q, b, :],
                                              AT[:, b, n0:n1], start=(b == 0 and q == 0),
                                              stop=(b == BLOCKS - 1 and q == PARTS - 1))
                mm.then_inc(acc_done, 1)
                if c:
                    finish(c - 1)
            finish(len(chunks) - 1)

        def general_finish_pe(pe):
            pe.wait_ge(acc_done, 1)
            for c, (n0, n1) in enumerate(chunks):
                if c >= 2:
                    pe.wait_ge(y_sb, SUPERS + c - 1)
                pe.wait_ge(agg_done, c + 1)
                for b, n in enumerate(range(n0, n1, BLOCK)):
                    m = min(BLOCK, n1 - n)
                    for i, (rows, w) in enumerate(((x1T[:, n:n + m], w1T),
                                                   (aggT[:, c % 2, b * BLOCK:b * BLOCK + m], w2T))):
                        mm = nc.tensor.matmul(ps[0:m, (2 + c % 2) * BANK + b * D:(2 + c % 2) * BANK + (b + 1) * D],
                                              rows, w[:, :], start=(i == 0), stop=(i == 1))
                mm.then_inc(o_done, 1)

        def final_sp(sp):
            res = [x_in, y]
            for c, (n0, n1) in enumerate(chunks):
                k = (n1 - n0 + BLOCK - 1) // BLOCK
                if c >= 2:
                    sp.wait_ge(y_sb, SUPERS + c - 1)
                sp.dma_start(res[c % 2][:, 0:k, :], x1_dram[n0:n0 + k * BLOCK, :]
                             .rearrange("(k p) d -> p k d", p=BLOCK)).then_inc(x1_back[c % 2], 16)
                if c >= 1:
                    store(sp, c - 1)
            store(sp, len(chunks) - 1)
            sp.wait_ge(stored, 16 * len(chunks))

        def store(sp, c):
            n0, n1 = chunks[c]
            k, m = -(-(n1 - n0) // BLOCK), min(BLOCK, n1 - n0)
            sp.wait_ge(fin_done, c + 1)
            sp.dma_start(out[n0:n1, :].rearrange("(k p) d -> p k d", p=m), x1s[0:m, 0:k, :]).then_inc(stored, 16)

        def final_dve(dve, norm, c):
            n0, n1 = chunks[c]
            m, k = min(BLOCK, n1 - n0), -(-(n1 - n0) // BLOCK)
            res = (x_in, y)[c % 2]
            dve.wait_ge(o_done, c + 1)
            dve.wait_ge(res_done, c + 1)
            nc.vector.tensor_tensor(res[0:m, 0:k, :], res[0:m, 0:k, :],
                                    ps[0:m, (2 + c % 2) * BANK:(2 + c % 2) * BANK + k * D]
                                    .rearrange("p (k d) -> p k d", d=D), ALU.add).then_inc(y_sb, 1)
            dve.wait_ge(y_sb, SUPERS + c + 1)
            if c:
                dve.wait_ge(stored, 16 * c)
            norm(res, x1s, m, k, SUPERS + c, fin_done)

        @block.sync
        def _(sp):
            for to, of in key_loads:
                sp.dma_start(to, of).then_inc(keys_loaded, 16)
            sp.wait_ge(consts, 1)
            for to, of in weights:
                sp.dma_start(to, of).then_inc(loads, 16)
            sp.wait_ge(flag_done, 1)
            f = sp.value_load(flag[0:1, 0:1], min_val=0, max_val=1 << 20)
            with sp.If(f > 0):
                general_sp(sp, 0)
            with sp.Else():
                edges_sp(sp)
            for b in range(SUPERS):
                if b == 0:
                    sp.wait_ge(sums_done, 1)
                else:
                    sp.wait_ge(y_sb, b)
                sp.dma_start(x_in, x[b * SNODES:(b + 1) * SNODES, :].rearrange("(k p) d -> p k d", p=BLOCK))\
                    .then_inc(x_loaded, 16)
                sp.wait_ge(x1_done, b + 1)
                sp.dma_start(x1_dram[b * SNODES:(b + 1) * SNODES, :].rearrange("(k p) d -> p k d", p=BLOCK),
                             x1s).then_inc(x1_stored, 16)
            sp.wait_ge(x1_stored, 16 * SUPERS)
            with sp.If(f > 0):
                general_sp(sp, 1)
            with sp.Else():
                sp.wait_ge(lo_done, SUPERS)
            final_sp(sp)

        @block.gpsimd
        def _(pool):
            nc.gpsimd.iota(iota[:, 0:WCOLS], [[1, WCOLS]], base=0, channel_multiplier=0,
                           allow_small_or_imprecise_dtypes=True).then_inc(pool_consts, 1)
            nc.gpsimd.memset(ident[:, :], 0.0).then_inc(pool_consts, 1)
            nc.gpsimd.iota(node_iota, [[1, NODES]], base=0, channel_multiplier=0,
                           allow_small_or_imprecise_dtypes=True).then_inc(pool_consts, 1)
            pool.wait_ge(pool_consts, 3)
            nc.gpsimd.affine_select(out=ident[:, :], in_=ident[:, :], compare_op=ALU.not_equal, fill=1.0, base=0,
                                    pattern=[[-1, P]], channel_multiplier=1).then_inc(pool_consts, 1)
            pool.wait_ge(flag_done, 1)
            f = pool.value_load(flag[0:1, 0:1], min_val=0, max_val=1 << 20)
            with pool.If(f > 0):
                general_pool(pool, 0)
            with pool.Else():
                edges_pool(pool)
            pool.wait_ge(x1_stored, 16 * SUPERS)
            with pool.If(f > 0):
                general_pool(pool, 1)
            with pool.Else():
                pool.wait_ge(x1_stored, 16 * SUPERS)
            res = [x_in, y]
            for c, (n0, n1) in enumerate(chunks):
                k = (n1 - n0 + BLOCK - 1) // BLOCK
                pool.wait_ge(x1_back[c % 2], 16 * (c // 2 + 1))
                for b in range(k):
                    ins = nc.gpsimd.tensor_tensor(res[c % 2][:, b, :], res[c % 2][:, b, :], biasO[:, :], ALU.add)
                ins.then_inc(res_done, 1)

        @block.scalar
        def _(act):
            act.wait_ge(consts, 2)
            nc.scalar.activation(tmp1[:, 1, :], tmp1[:, 0, :], ACT.Sqrt).then_inc(achain, 1)
            nc.scalar.activation(tmp2[:, 1, :], tmp2[:, 0, :], ACT.Sqrt).then_inc(achain, 1)
            act.wait_ge(keys_done, 1)
            f = act.value_load(flag[0:1, 0:1], min_val=0, max_val=1 << 20)
            with act.If(f > 0):
                general_act(act)
            with act.Else():
                edges_act(act)
            act.wait_ge(sums_done, 1)
            for b in range(SUPERS):
                act.wait_ge(z_done, b + 1)
                if b:
                    act.wait_ge(y_done, b)
                for h in range(HALVES):
                    for lo, hi in parts:
                        ins = nc.scalar.activation(rT[:, h, lo * BLOCK:hi * BLOCK], psZ[h][lo > 0], ACT.Relu,
                                                   bias=bias1[:, h:h + 1], scale=scale1[:, h:h + 1])
                ins.then_inc(r_done, 1)
                act.wait_ge(var_done, b + 1)
                nc.scalar.activation(std[:, :], mean_var[:, :, 1], ACT.Sqrt, bias=epsc[:, 0:1]).then_inc(std_done, 1)
                act.wait_ge(x1_done, b + 1)
                nc.scalar.copy(x1p[:, 0, b * SPAN:(b + 1) * SPAN, :], x1s).then_inc(hi_done, 1)
                act.wait_ge(rest_done, b + 1)
                nc.scalar.copy(x1p[:, 1, b * SPAN:(b + 1) * SPAN, :], y).then_inc(mid_done, 1)
                act.wait_ge(xt_done, b + 1)
                for lo, hi in parts:
                    ins = nc.scalar.copy(x1T[:, b * SNODES + lo * BLOCK:b * SNODES + hi * BLOCK], psT[lo > 0])
                ins.then_inc(x1T_done, 1)
            for c, (n0, n1) in enumerate(chunks):
                act.wait_ge(var_done, SUPERS + c + 1)
                m, k = min(BLOCK, n1 - n0), -(-(n1 - n0) // BLOCK)
                nc.scalar.activation(std[0:m, 0:k], mean_var[0:m, 0:k, 1], ACT.Sqrt, bias=epsc[0:m, 0:1])\
                    .then_inc(std_done, 1)

        @block.vector
        def _(dve):
            count = [0]

            def link(ins):
                count[0] += 1
                ins.then_inc(vchain, 1)
                dve.wait_ge(vchain, count[0])

            def norm(src, to, m, k, n, done):
                for b in range(k):
                    ins = nc.vector.bn_stats(stats[0:m, b, :], src[0:m, b, :])
                link(ins)
                if n:
                    dve.wait_ge(std_done, n)
                for b in range(k):
                    ins = nc.vector.bn_aggr(mean_var[0:m, b, :], stats[0:m, b, :])
                ins.then_inc(var_done, 1)
                dve.wait_ge(std_done, n + 1)
                link(nc.vector.reciprocal(rstd[0:m, 0:k], std[0:m, 0:k]))
                for b in range(k):
                    ins = nc.vector.tensor_scalar(to[0:m, b, :], src[0:m, b, :], mean_var[0:m, b, 0:1],
                                                  rstd[0:m, b:b + 1], ALU.subtract, ALU.mult)
                ins.then_inc(done, 1)

            for s, n in ((e_done, 2), (sum_done, 4), (p_done, 4), (added, 2), (mv_used, 4), (a_done, 2),
                         (copied, 2)):
                dve.sem_inc(s, n)
            nc.vector.memset(ones[:, :], 1.0)
            nc.vector.memset(viol[:, :], 0.0)
            nc.vector.memset(ef[0:EF + 1, :, :], 1.0)
            nc.vector.memset(ob_last[:, UNROLL - 1, :], 0.0)
            nc.vector.memset(hT[:, ROWS:], 0.0)
            nc.vector.memset(unit_row[:, 0:EF], 0.0)
            nc.vector.memset(unit_row[:, EF:EF + 1], 1.0)
            link(nc.vector.memset(epsc[:, :], LN_EPS))
            nc.vector.memset(c_key[:, 0:1], -1.0).then_inc(consts, 1)
            dve.wait_ge(keys_loaded, 16 * len(key_loads))
            link(nc.vector.tensor_tensor(t_f, dst_ai, dst_bi, ALU.is_gt))
            link(nc.vector.tensor_reduce(viol[:, 0:1], t_f, AX_X, ALU.add))
            link(nc.vector.tensor_tensor(t_g[0:1, :], last_i[0:1, :], base_b[0:1, :], ALU.subtract))
            link(nc.vector.tensor_scalar(t_g[0:1, :], t_g[0:1, :], float(WIN - 1), None, ALU.is_gt))
            link(nc.vector.tensor_reduce(viol[0:1, 1:2], t_g[0:1, :], AX_X, ALU.add))
            link(nc.vector.tensor_tensor(t_g[0:1, 0:GROUPS - 1], third_i[0:1, 0:GROUPS - 1],
                                         base_b[0:1, 1:GROUPS], ALU.is_ge))
            link(nc.vector.tensor_reduce(viol[0:1, 2:3], t_g[0:1, 0:GROUPS - 1], AX_X, ALU.add))
            link(nc.vector.tensor_tensor(t_g[0:1, 1:GROUPS], base_b[0:1, 1:GROUPS], base_b[0:1, 0:GROUPS - 1],
                                         ALU.subtract))
            link(nc.vector.tensor_scalar(t_g[0:1, 1:GROUPS], t_g[0:1, 1:GROUPS], float(WIN), None, ALU.is_gt))
            link(nc.vector.tensor_scalar(t_g[0:1, 0:1], base_b[0:1, 0:1], 0.0, None, ALU.not_equal))
            link(nc.vector.tensor_reduce(viol[0:1, 3:4], t_g[0:1, :], AX_X, ALU.add))
            link(nc.vector.tensor_reduce(t_f[:, 0:1], viol[:, :], AX_X, ALU.add))
            nc.vector.memset(t_g[:, 0:1], 0.0).then_inc(viol_done, 1)
            dve.wait_ge(viol_sum, 1)
            nc.vector.tensor_copy(flag[:, :], psE[1][0:1, 0:1]).then_inc(flag_done, 1)
            link(nc.vector.tensor_scalar(t_i, src_i, 7, None, ALU.logical_shift_right))
            link(nc.vector.tensor_copy(a_f, t_i))
            link(nc.vector.tensor_scalar(t_i, src_i, BLOCK - 1, None, ALU.bitwise_and))
            link(nc.vector.tensor_copy(b_key, t_i))
            by_group = base_b.unsqueeze(2).to_broadcast([P, GROUPS, GROUP])
            link(nc.vector.tensor_tensor(d_key.rearrange("p (g j) -> p g j", j=GROUP),
                                         dst_i.rearrange("p (g j) -> p g j", j=GROUP), by_group, ALU.subtract))
            link(nc.vector.scalar_tensor_tensor(out=m_key, in0=a_f, scalar=float(WIN), in1=d_key,
                                                op0=ALU.mult, op1=ALU.add))
            def last_tiles(a):
                return a.rearrange("p (g j) -> p g j", j=GROUP)[:, 0:GROUPS - 1, GROUP - 1]
            link(nc.vector.tensor_tensor(t_g[:, 1:GROUPS], last_tiles(dst_i), base_b[:, 1:GROUPS], ALU.not_equal))
            link(nc.vector.scalar_tensor_tensor(out=c_key[:, 1:GROUPS], in0=t_g[:, 1:GROUPS], scalar=64.0,
                                                in1=last_tiles(a_f), op0=ALU.mult, op1=ALU.add))
            link(nc.vector.tensor_copy(dst_f, dst_i))
            dve.wait_ge(loads, 16 * len(weights))
            link(nc.vector.tensor_scalar(eps1p[:, :], eps1[:, :], 1.0, None, ALU.add))
            first_of_act = count[0]
            link(nc.vector.tensor_scalar(hT[:, 0:ROWS], hT[:, 0:ROWS], eps1p[:, 0:1], None, ALU.mult))
            link(nc.vector.tensor_scalar(tmp1[:, 0, :], bn1[:, 4, :], BN_EPS, None, ALU.add))
            link(nc.vector.tensor_scalar(tmp2[:, 0, :], bn2[:, 4, :], BN_EPS, None, ALU.add))
            nc.vector.memset(t_g[:, 0:1], 0.0).then_inc(consts, 1)
            dve.wait_ge(achain, 2)
            link(nc.vector.reciprocal(tmp1[:, 2, :], tmp1[:, 1, :]))
            link(nc.vector.reciprocal(tmp2[:, 2, :], tmp2[:, 1, :]))
            link(nc.vector.tensor_tensor(scale1[:, :], tmp1[:, 2, :], bn1[:, 1, :], ALU.mult))
            link(nc.vector.tensor_tensor(scale2[:, :], tmp2[:, 2, :], bn2[:, 1, :], ALU.mult))
            link(nc.vector.tensor_tensor(tmp1[:, 3, :], bn1[:, 0, :], bn1[:, 3, :], ALU.subtract))
            link(nc.vector.tensor_tensor(tmp2[:, 3, :], bn2[:, 0, :], bn2[:, 3, :], ALU.subtract))
            link(nc.vector.tensor_tensor(tmp1[:, 0, :], tmp1[:, 3, :], scale1[:, :], ALU.mult))
            link(nc.vector.tensor_tensor(tmp2[:, 0, :], tmp2[:, 3, :], scale2[:, :], ALU.mult))
            link(nc.vector.tensor_tensor(bias1[:, :], tmp1[:, 0, :], bn1[:, 2, :], ALU.add))
            link(nc.vector.tensor_tensor(bias2[:, :], tmp2[:, 0, :], bn2[:, 2, :], ALU.add))
            link(nc.vector.tensor_tensor(biasO[:, :], outb[:, 0, :], outb[:, 1, :], ALU.add))
            for h in range(HALVES):
                link(nc.vector.tensor_tensor(wm2[:, h, :], wm2[:, h, :], scale2[:, :], ALU.mult))
            dve.wait_ge(wc_done, 1)
            link(nc.vector.tensor_copy(wc[:, :], psE[0][0:EF + 1, 0:D]))
            nc.vector.memset(t_g[:, 0:1], 0.0).then_inc(wc_ready, 1)
            dve.wait_ge(pool_consts, 4)
            dve.sem_inc(keys_done, 1)
            f = dve.value_load(flag[0:1, 0:1], min_val=0, max_val=1 << 20)
            with dve.If(f > 0):
                general_dve(dve, 0)
                nc.vector.tensor_tensor(hT[:, 0:NODES], hT[:, 0:NODES], ps[:, 0:NODES], ALU.add)\
                    .then_inc(sums_done, 1)
            with dve.Else():
                edges_dve(dve)
                dve.wait_ge(added, GROUPS + 2)
                dve.wait_ge(copied, GROUPS + 2)
                dve.sem_inc(sums_done, 1)
            for b in range(SUPERS):
                dve.wait_ge(x_loaded, 16 * (b + 1))
                for k in range(SPAN):
                    ins = nc.vector.tensor_tensor(x_in[:, k, :], x_in[:, k, :], bias2[:, :], ALU.add)
                link(ins)
                dve.wait_ge(y_done, b + 1)
                for lo, hi in parts:
                    ins = nc.vector.tensor_tensor(
                        y[:, lo:hi, :], psY[:, lo * D:hi * D].rearrange("p (k d) -> p k d", d=D),
                        x_in[:, lo:hi, :], ALU.add)
                ins.then_inc(y_sb, 1)
                dve.wait_ge(y_sb, b + 1)
                if b:
                    dve.wait_ge(x1_stored, 16 * b)
                    dve.wait_ge(xt_done, b)
                norm(y, x1s, P, SPAN, b, x1_done)
                dve.wait_ge(hi_done, b + 1)
                nc.vector.tensor_tensor(y, x1s, x1p[:, 0, b * SPAN:(b + 1) * SPAN, :], ALU.subtract)\
                    .then_inc(rest_done, 1)
                dve.wait_ge(mid_done, b + 1)
                nc.vector.tensor_tensor(x1p[:, 2, b * SPAN:(b + 1) * SPAN, :], y,
                                        x1p[:, 1, b * SPAN:(b + 1) * SPAN, :], ALU.subtract).then_inc(lo_done, 1)
                dve.wait_ge(lo_done, b + 1)
            before = count[0]
            with dve.If(f > 0):
                dve.wait_ge(x1T_done, SUPERS)
                general_dve(dve, 1)
                nc.vector.tensor_copy(hot, ps[:, 0:NODES]).then_inc(acc_done, 1)
                dve.wait_ge(acc_done, 1)
                for c, (n0, n1) in enumerate(chunks):
                    if c >= 2:
                        dve.wait_ge(o_done, c - 1)
                    nc.vector.tensor_copy(aggT[:, c % 2, 0:n1 - n0], hot[:, n0:n1]).then_inc(agg_done, 1)
                    final_dve(dve, norm, c)
            with dve.Else():
                count[0] = before
                for c, (n0, n1) in enumerate(chunks):
                    dve.wait_ge(acc_done, c + 1)
                    if c >= 2:
                        dve.wait_ge(o_done, c - 1)
                    nc.vector.tensor_copy(aggT[:, c % 2, 0:n1 - n0], ps[:, (c % 2) * BANK:(c % 2) * BANK + n1 - n0])\
                        .then_inc(agg_done, 1)
                    final_dve(dve, norm, c)
            dve.wait_ge(fin_done, len(chunks))

        @block.tensor
        def _(pe):
            pe.wait_ge(viol_done, 1)
            nc.tensor.matmul(psE[1][0:1, 0:1], t_f[:, 0:1], ones[:, :], start=True, stop=True).then_inc(viol_sum, 1)
            pe.wait_ge(loads, 16 * len(weights))
            for h in range(HALVES):
                nc.tensor.matmul(psE[0][0:EF + 1, 0:D], we1T[:, h, :], we2[:, h, :], start=(h == 0), stop=False)
            nc.tensor.matmul(psE[0][0:EF + 1, 0:D], unit_row, be2_row, start=False, stop=True).then_inc(wc_done, 1)
            pe.wait_ge(wc_ready, 1)
            pe.wait_ge(keys_done, 1)
            f = pe.value_load(flag[0:1, 0:1], min_val=0, max_val=1 << 20)
            with pe.If(f > 0):
                general_pe(pe, 0)
            with pe.Else():
                edges_pe(pe)
            pe.wait_ge(sums_done, 1)
            for b in range(SUPERS):
                if b:
                    pe.wait_ge(r_done, b)
                for h in range(HALVES):
                    for lo, hi in parts:
                        mm = nc.tensor.matmul(psZ[h][lo > 0], wm1[:, h * P:(h + 1) * P],
                                              hT[:, b * SNODES + lo * BLOCK:b * SNODES + hi * BLOCK],
                                              start=True, stop=True)
                mm.then_inc(z_done, 1)
                pe.wait_ge(r_done, b + 1)
                if b:
                    pe.wait_ge(y_sb, b)
                for k in range(SPAN):
                    for h in range(HALVES):
                        mm = nc.tensor.matmul(psY[:, k * D:(k + 1) * D], rT[:, h, k * BLOCK:(k + 1) * BLOCK],
                                              wm2[:, h, :], start=(h == 0), stop=(h == HALVES - 1))
                mm.then_inc(y_done, 1)
                pe.wait_ge(x1_done, b + 1)
                if b:
                    pe.wait_ge(x1T_done, b)
                for k in range(SPAN):
                    p, at = int(k >= LOW), (k - LOW * (k >= LOW)) * BLOCK
                    mm = nc.tensor.transpose(psT[p][:, at:at + BLOCK], x1s[:, k, :], ident[:, :])
                mm.then_inc(xt_done, 1)
            pe.wait_ge(x1T_done, SUPERS)
            with pe.If(f > 0):
                general_pe(pe, 1)
                general_finish_pe(pe)
            with pe.Else():
                aggregate_pe(pe)
            pe.wait_ge(fin_done, len(chunks))


def kernel(x, src, dst, edge_attr_16, L0_gnn_We1, L0_gnn_be1, L0_gnn_We2, L0_gnn_be2, L0_gnn_eps, L0_gnn_Wm1,
           L0_gnn_bm1, L0_gnn_g1, L0_gnn_b1, L0_gnn_m1, L0_gnn_v1, L0_gnn_Wm2, L0_gnn_bm2, L0_gnn_g2, L0_gnn_b2,
           L0_gnn_m2, L0_gnn_v2, L1_gnn_W1, L1_gnn_b1, L1_gnn_W2, L1_gnn_b2):
    import numpy as np
    import concourse.bacc as bacc
    from concourse.bass_utils import run_bass_kernel_spmd

    def filled(a, rows, value):
        a = np.asarray(a)
        return np.concatenate([a, np.full((rows - len(a), *a.shape[1:]), value, a.dtype)])

    def tiles(a):
        return np.ascontiguousarray(a.reshape(TILES, P).T)

    def halves(a):
        return np.ascontiguousarray(np.asarray(a).reshape(HALVES, P).T)

    def row(a):
        return np.ascontiguousarray(np.asarray(a).reshape(1, -1))

    n = TILES * P
    src_p, dst_p = filled(src, n, 0), filled(dst, n + 1, NODES)
    x_p = filled(x, ROWS, 0)
    data = {
        "x": x_p, "xT": np.ascontiguousarray(x_p.T), "src_t": tiles(src_p), "dst_t": tiles(dst_p[:n]),
        "dst_a": dst_p[:n].reshape(P, TILES), "dst_b": dst_p[1:].reshape(P, TILES),
        "first": row(dst_p[0:n:GEDGES]), "last": row(dst_p[GEDGES - 1:n:GEDGES]),
        "third": row(dst_p[GEDGES - P - 1:n:GEDGES]),
        "efT": np.ascontiguousarray(filled(edge_attr_16, n, 0).T),
        "We1T": np.ascontiguousarray(np.concatenate([np.asarray(L0_gnn_We1), row(L0_gnn_be1)]).T),
        "We2": np.asarray(L0_gnn_We2), "be2": row(L0_gnn_be2), "eps": row(L0_gnn_eps),
        "Wm1": np.asarray(L0_gnn_Wm1), "bm1": halves(L0_gnn_bm1), "g1": halves(L0_gnn_g1), "b1": halves(L0_gnn_b1),
        "m1": halves(L0_gnn_m1), "v1": halves(L0_gnn_v1), "Wm2": np.asarray(L0_gnn_Wm2), "bm2": row(L0_gnn_bm2),
        "g2": row(L0_gnn_g2), "b2": row(L0_gnn_b2), "m2": row(L0_gnn_m2), "v2": row(L0_gnn_v2),
        "W1T": np.ascontiguousarray(np.asarray(L1_gnn_W1).T), "bb1": row(L1_gnn_b1),
        "W2T": np.ascontiguousarray(np.asarray(L1_gnn_W2).T), "bb2": row(L1_gnn_b2),
    }
    nc = bacc.Bacc("TRN2", target_bir_lowering=False, num_devices=1)
    arrays, args = {}, []
    for name, a in data.items():
        arrays[f"in_{name}"] = a
        args.append(nc.dram_tensor(f"in_{name}", a.shape, mybir.dt.from_np(a.dtype), kind="ExternalInput").ap())
    args.append(nc.dram_tensor("out_0", (NODES, D), F32, kind="ExternalOutput").ap())
    args.append(nc.dram_tensor("x1_rows", (ROWS, D), F32, kind="Internal").ap())
    gnn_kernel(nc, *args)
    result = run_bass_kernel_spmd(nc, [arrays], core_ids=[0])
    return result.results[0]["out_0"]
```

```python
from contextlib import ExitStack

import concourse.bass as bass
from concourse import mybir

F32 = mybir.dt.float32
I32 = mybir.dt.int32
F16 = mybir.dt.float16
BF16 = mybir.dt.bfloat16
ALU = mybir.AluOpType
ACT = mybir.ActivationFunctionType
AX_X = mybir.AxisListType.X

NODES, D, HID, EF = 3125, 128, 256, 16
EDGES = 53125
P = 128
GROUP = 4
GEDGES = GROUP * P
GROUPS = -(-EDGES // GEDGES)
TILES = GROUPS * GROUP
UNROLL = 4
TURNS = GROUPS // UNROLL
BLOCK = 128
BLOCKS = -(-NODES // BLOCK)
ROWS = BLOCKS * BLOCK
BANK = 512
UNIT = BANK
UNITS = -(-ROWS // UNIT)
HALVES = HID // P
OROWS = 125
OUNIT = BANK // OROWS * OROWS
WIN = 39
CWIN = 14
CCOLS = BLOCKS * CWIN
PARTS = 3
FEATURE_PARTS, WEIGHT_PARTS = (0, 1, 2, 0, 1, 0), (0, 0, 0, 1, 1, 2)
ONES_AT = len(FEATURE_PARTS) * EF
STACK = ONES_AT + PARTS
PEDGES = 2 * GEDGES
SEGS = P // EF
SEG = PEDGES // SEGS
MARGIN = 2
BN_EPS, LN_EPS = 0.001, 1e-05

SPAN = 4
STEPS = SPAN * UNROLL

UNIT_TURN = {}
for m in range(UNITS):
    at = -(-(-(-(m + 1) * UNIT * EDGES // (NODES * GEDGES)) + MARGIN) // UNROLL)
    at = max([at] + [t + SPAN for t in UNIT_TURN.values()])
    if at + SPAN <= TURNS:
        UNIT_TURN[m] = at
LATE = [m for m in range(UNITS) if m not in UNIT_TURN]


def unit_blocks(m):
    return min(UNIT, ROWS - m * UNIT) // BLOCK


def segments():
    found, t = [(0, 1, None)], 1
    todo = sorted(UNIT_TURN)
    while todo:
        m = todo[0]
        if t < UNIT_TURN[m]:
            found.append((t, UNIT_TURN[m], None))
        n = m + 1
        while n in UNIT_TURN and UNIT_TURN[n] == UNIT_TURN[n - 1] + SPAN and UNIT_TURN[n] + SPAN < TURNS:
            n += 1
        found.append((UNIT_TURN[m], None, (m, n)))
        t = UNIT_TURN[n - 1] + SPAN
        todo = todo[n - m:]
    assert t == TURNS
    return found


def linear(n, scale=1, offset=0):
    def at(k, c=0):
        return n * (scale * k) + (offset * k + c)
    return at


def gnn_kernel(nc, x, xT, src_t, dst_t, dst_a, dst_b, first, spans, efT, wfix, wtmp, rows, out,
               x1_dram, res_dram):
    with ExitStack() as ctx:
        def sb(name, shape, dt=F32):
            return ctx.enter_context(nc.sbuf_tensor(name, shape, dt))

        def sem(name):
            return ctx.enter_context(nc.semaphore(name))

        ps = ctx.enter_context(nc.psum_tensor("ps", [P, 8 * BANK], F32))

        def bank(k, n=BANK):
            return ps[:, k * BANK:k * BANK + n]

        AT = sb("AT", [P, BLOCKS, NODES + CWIN + 1], F16)
        hT = sb("hT", [P, ROWS + WIN + 1])
        FEATURES = UNROLL * GROUP * D
        WORK = FEATURES + 3 * UNIT + (UNITS - 3) * PARTS * UNIT // 2
        work = sb("work", [P, WORK])

        class Carver:
            def __init__(self, ap, words):
                self.ap, self.at, self.words = ap, 0, words

            def take(self, words, dt=F32):
                a = self.ap[:, self.at:self.at + words]
                self.at += words
                assert self.at <= self.words
                return a if dt == F32 else a.bitcast(dt)

        edge = Carver(work, WORK)
        gath = edge.take(UNROLL * GROUP * D).rearrange("p (g j d) -> p g j d", g=UNROLL, j=GROUP)
        ef = edge.take(PEDGES, BF16).rearrange("p (k e) -> p k e", k=2)
        ef_d = edge.take(2 * SEG).rearrange("p (k c) -> p k c", k=2)
        ef_p = edge.take(PARTS * SEG, BF16).rearrange("p (k q c) -> p k q c", k=2, q=PARTS)
        mv = edge.take(GROUP * CCOLS // 2, F16).rearrange("p (j c) -> p j c", j=GROUP)
        ob = edge.take(2 * (GROUP - 1) * BLOCK // 2, F16).rearrange("p (g j b) -> p g j b", g=2, j=GROUP - 1)
        ob_last = edge.take(UNROLL * BLOCK // 2, F16).rearrange("p (g b) -> p g b", g=UNROLL)
        od = edge.take(2 * GROUP * WIN).rearrange("p (g j w) -> p g j w", g=2, j=GROUP)
        mvc = edge.take(GROUP * BLOCKS, F16).rearrange("p (g j a) -> p g j a", g=2, j=GROUP)
        b_key = edge.take(TILES // 2, F16)
        m_key = edge.take(TILES // 2, F16)
        d_key = edge.take(TILES // 2, F16)
        c_key = edge.take(TILES // 2, F16)
        iota = edge.take(CCOLS // 2, F16)

        xr = [work[:, FEATURES + k * UNIT:FEATURES + (k + 1) * UNIT] for k in range(2)]
        rest = work[:, FEATURES + 2 * UNIT:FEATURES + 3 * UNIT]
        X1P = PARTS * UNIT // 2
        X1P_AT = [0, X1P] + [FEATURES + 3 * UNIT + k * X1P for k in range(UNITS - 3)] + [2 * X1P]

        def x1p(q):
            nb = unit_blocks(q)
            return work[:, X1P_AT[q]:X1P_AT[q] + PARTS * nb * D // 2].bitcast(BF16)\
                .rearrange("p (k b d) -> p k b d", k=PARTS, b=nb)

        NO_BLOCK = 64.0
        assert NO_BLOCK >= BLOCKS
        SCRATCH = 16000
        AT_w = AT[:, :, :].rearrange("p a n -> p (a n)")[:, 0:2 * SCRATCH].bitcast(F32)
        early = Carver(AT_w, SCRATCH)
        src_i = early.take(TILES, I32)
        dst_i = early.take(TILES, I32)
        dst_ai = early.take(TILES, I32)
        dst_bi = early.take(TILES, I32)
        base_t = early.take(TILES, I32)
        t_i = early.take(TILES, I32)
        a_f = early.take(TILES)
        t_f = early.take(TILES)
        spans_t = early.take(4 * GROUP + 2, I32)[0:GROUPS, :]
        diffs = early.take(2 * GROUP + 1)[0:GROUPS, :]
        chk = early.take(3 * GROUP + 3)[0:GROUPS, :]
        wt = early.take(HALVES * (STACK + D + 1))
        we1T = wt[:, 0:HALVES * STACK].rearrange("p (h e) -> p h e", h=HALVES)
        we2 = wt[:, HALVES * STACK:HALVES * (STACK + D)].rearrange("p (h d) -> p h d", h=HALVES)
        less = wt[:, HALVES * (STACK + D):]
        unit_row = early.take(STACK)[0:1, :]
        wc_part = early.take(D // 2, BF16)[0:STACK, :]
        wc_rest = early.take(D)[0:STACK, :]
        general = Carver(AT_w, SCRATCH)
        general.take(early.at)
        hot = general.take(NODES)
        dst_f = general.take(TILES)
        node_iota = general.take(NODES)
        ef_g = general.take(GEDGES)
        wc_g = general.take(D)

        x_in = sb("x_in", [P, UNIT // BLOCK, D])
        x1s = sb("x1s", [P, UNIT // BLOCK, D])
        rT = sb("rT", [P, HALVES, UNIT])
        x1T = rT[:, 0, :]
        aggT = rT
        stats = sb("stats", [P, UNIT // BLOCK, 6])
        mean_var = sb("mean_var", [P, UNIT // BLOCK, 2])
        std = sb("std", [P, UNIT // BLOCK])
        rstd = sb("rstd", [P, UNIT // BLOCK])

        rw = rT[:, :, :].rearrange("p h n -> p (h n)")
        bm2, g2, b2, m2, v2, bb1, bb2, be2 = [rw[:, k * D:(k + 1) * D] for k in range(8)]
        tmp2 = x1s[:, :, :]
        scale2, brow_f, brow_part = x_in[:, 0, :], x_in[0:PARTS, 1:3, :], x_in[0:PARTS, 3, :].bitcast(BF16)\
            .rearrange("p (k d) -> p k d", k=2)

        wf = sb("wf", [P, HID + HALVES * D + 2 * D + 6 * HALVES])
        wm1 = wf[:, 0:HID]
        wm2 = wf[:, HID:HID + HALVES * D].rearrange("p (h d) -> p h d", h=HALVES)
        w1T = wf[:, HID + HALVES * D:HID + HALVES * D + D]
        w2T = wf[:, HID + HALVES * D + D:HID + HALVES * D + 2 * D]
        bm1, g1, b1, m1, v1, less_b = [wf[:, HID + HALVES * D + 2 * D + HALVES * k:
                                          HID + HALVES * D + 2 * D + HALVES * (k + 1)] for k in range(6)]
        tmp1 = sb("tmp1", [P, 4, HALVES])
        wc = sb("wc", [STACK, D], BF16)
        brow = sb("brow", [PARTS, 3, P], BF16)
        scale1 = sb("scale1", [P, HALVES])
        bias1 = sb("bias1", [P, HALVES])
        eps1p = sb("eps1p", [P, 1])
        epsc = sb("epsc", [P, 1])
        epsb = sb("epsb", [P, 1])
        ones = sb("ones", [P, 1])
        viol = sb("viol", [P, 2])
        flag = sb("flag", [1, 1], I32)
        bases = sb("bases", [1, TILES], I32)
        idx = sb("idx", [P, UNROLL, GROUP], I32)
        ident = sb("ident", [P, P])

        flag_loads = sem("flag_loads")
        key_loads = sem("key_loads")
        weights = sem("weights")
        loads = sem("loads")
        pool_consts = sem("pool_consts")
        consts = sem("consts")
        vchain = sem("vchain")
        viol_done = sem("viol_done")
        viol_sum = sem("viol_sum")
        flag_done = sem("flag_done")
        norm_stds = sem("norm_stds")
        norm_chain = sem("norm_chain")
        eps_done = sem("eps_done")
        h_loaded = sem("h_loaded")
        h_scaled = sem("h_scaled")
        keys_done = sem("keys_done")
        wc_done = sem("wc_done")
        efd_in = [sem(f"efd_in{k}") for k in range(2)]
        ef_hi = sem("ef_hi")
        ef_rest = sem("ef_rest")
        ef_mid = sem("ef_mid")
        ef_lo = sem("ef_lo")
        ef_in = [sem(f"ef_in{k}") for k in range(2)]
        idx_in = [sem(f"idx_in{k}") for k in range(UNROLL)]
        gathered = [sem(f"gathered{k}") for k in range(UNROLL)]
        pool_step = sem("pool_step")
        e_done = sem("e_done")
        sum_done = sem("sum_done")
        msg_done = sem("msg_done")
        od_done = sem("od_done")
        p_done = sem("p_done")
        added = sem("added")
        ob_done = sem("ob_done")
        mv_done = sem("mv_done")
        mvc_done = sem("mvc_done")
        mv_used = sem("mv_used")
        a_done = sem("a_done")
        copied = sem("copied")
        START = {**{s: 16 for s in idx_in[1:]}, e_done: 2, sum_done: 4, p_done: 4, added: 2, mv_used: 4, a_done: 8,
                 copied: 2}
        x_loaded = sem("x_loaded")
        z_done = sem("z_done")
        r_done = sem("r_done")
        y_done = sem("y_done")
        y_sb = sem("y_sb")
        stats_done = sem("stats_done")
        dve_step = sem("dve_step")
        var_done = sem("var_done")
        std_done = sem("std_done")
        rstd_done = sem("rstd_done")
        x1_done = sem("x1_done")
        x1_stored = sem("x1_stored")
        xt_done = sem("xt_done")
        x1T_done = sem("x1T_done")
        o1_done = sem("o1_done")
        res_done = sem("res_done")
        res_stored = sem("res_stored")
        START_UNITS = {r_done: 1, std_done: 1, xt_done: 1, x1T_done: 1, o1_done: 1, res_done: 1, x1_stored: 16,
                       res_stored: 16}
        xr_in = [sem(f"xr_in{k}") for k in range(2)]
        hi_done = sem("hi_done")
        rest_done = sem("rest_done")
        mid_done = sem("mid_done")
        lo_done = sem("lo_done")
        acc_done = sem("acc_done")
        agg_done = sem("agg_done")
        o_done = sem("o_done")
        res_in = [sem(f"res_in{k}") for k in range(2)]
        f_sb = sem("f_sb")
        f_stats = sem("f_stats")
        f_var = sem("f_var")
        f_std = sem("f_std")
        f_rstd = sem("f_rstd")
        fin_done = sem("fin_done")
        stored = [sem(f"stored{k}") for k in range(2)]
        acc_zero = sem("acc_zero")
        added_all = sem("added_all")
        G = [{n: sem(f"g{n}{layer}") for n in ("idx", "ef", "gath", "e", "sum", "msg", "hot", "used", "turn")}
             for layer in range(2)]

        psE, psP, psA = bank(0), [bank(1, WIN), bank(7, WIN)], [bank(2, CCOLS), bank(3, CCOLS)]
        psZ, psY = [bank(4), bank(5)], bank(6)
        psT = psZ[0]
        psAcc, psO = [bank(k) for k in (2, 3, 0, 1)], psZ
        gE = bank(7)
        banks = [(n, min(n + BANK, NODES)) for n in range(0, NODES, BANK)]
        chunks = [(n, min(n + OUNIT, NODES)) for n in range(0, NODES, OUNIT)]

        block = ctx.enter_context(nc.Block())

        def general_sp(sp, layer):
            s = G[layer]
            for u in range(UNROLL):
                sp.wait_ge(gathered[u], 16 * GROUP)
            sp.wait_ge(consts, 2)
            with sp.Fori(0, GROUPS) as g:
                sp.wait_ge(s["turn"], g + 1)
                sp.dma_start(idx[:, 0, :], src_t[:, bass.ds(g * GROUP, GROUP)]).then_inc(s["idx"], 16)
                if layer == 0:
                    sp.dma_start(ef_g[0:EF, :], efT[:, bass.ds(g * GEDGES, GEDGES)]).then_inc(s["ef"], 16)

        def general_pool(pool, layer):
            s, table = G[layer], (x, x1_dram)[layer]
            if layer == 0:
                pool.wait_ge(keys_done, 1)
                for u in range(UNROLL):
                    pool.wait_ge(gathered[u], 16 * GROUP)
                nc.gpsimd.iota(node_iota, [[1, NODES]], base=0, channel_multiplier=0,
                               allow_small_or_imprecise_dtypes=True).then_inc(pool_consts, 1)
            with pool.Fori(0, GROUPS) as g:
                pool.wait_ge(s["idx"], g * 16 + 16)
                pool.sem_inc(pool_step, 1)
                for j in range(GROUP):
                    pool.indirect_dma_start(gath[:, 0, j, :], None, table,
                                            bass.IndirectOffsetOnAxis(idx[:, 0, j:j + 1], 0)).then_inc(s["gath"], 16)

        def general_pe(pe, layer):
            s = G[layer]
            pe.wait_ge(acc_zero, layer + 1)
            pe.sem_inc(s["turn"], 1)
            with pe.Fori(0, GROUPS) as g:
                if layer == 0:
                    pe.wait_ge(s["ef"], g * 16 + 16)
                    for j in range(GROUP):
                        mm = nc.tensor.matmul(gE[:, j * D:(j + 1) * D], ef_g[0:ONES_AT + 1, j * P:(j + 1) * P],
                                              wc_g[0:ONES_AT + 1, :], start=True, stop=True)
                    mm.then_inc(s["e"], 1)
                    pe.wait_ge(s["msg"], g + 1)
                else:
                    pe.wait_ge(s["gath"], g * (16 * GROUP) + 16 * GROUP)
                for j in range(GROUP):
                    pe.wait_ge(s["hot"], g * GROUP + (j + 1))
                    for c, e in banks:
                        mm = nc.tensor.matmul(ps[:, c:e], gath[:, 0, j, :], hot[:, c:e], start=False, stop=True,
                                              skip_group_check=True)
                    mm.then_inc(s["used"], 1)
                nc.tensor.matmul(gE[0:1, 0:1], ones[:, :], ones[:, :], start=True, stop=True).then_inc(s["turn"], 1)

        def general_dve(dve, layer):
            s = G[layer]
            if layer == 0:
                nc.vector.memset(ef_g[0:ONES_AT, :], 0.0)
                nc.vector.memset(ef_g[ONES_AT:ONES_AT + 1, :], 1.0)
                nc.vector.tensor_copy(wc_g[0:STACK, :], psE[0:STACK, 0:D])
                nc.vector.tensor_copy(dst_f, dst_i).then_inc(consts, 1)
                dve.wait_ge(consts, 2)
                dve.wait_ge(pool_consts, 4)
                dve.wait_ge(h_scaled, len(H_CUTS) - 1)
            nc.vector.memset(ps[:, :], 0.0).then_inc(acc_zero, 1)
            dve.sem_inc(s["used"], 1)
            with dve.Fori(0, GROUPS) as g:
                if layer == 0:
                    dve.wait_ge(s["e"], g + 1)
                    dve.wait_ge(s["gath"], g * (16 * GROUP) + 16 * GROUP)
                    nc.vector.tensor_tensor(gath[:, 0, :, :], gE.rearrange("p (j d) -> p j d", j=GROUP),
                                            gath[:, 0, :, :], ALU.add).then_inc(s["sum"], 1)
                for j in range(GROUP):
                    dve.wait_ge(s["used"], g * GROUP + (j + 1))
                    nc.vector.tensor_scalar(hot, node_iota, dst_f[:, bass.ds(g * GROUP + j, 1)], None,
                                            ALU.is_equal).then_inc(s["hot"], 1)
            dve.wait_ge(s["used"], TILES + 1)
            if layer == 0:
                nc.vector.tensor_tensor(hT[:, 0:NODES], hT[:, 0:NODES], ps[:, 0:NODES], ALU.add)\
                    .then_inc(added_all, 1)
            else:
                nc.vector.tensor_copy(hot, ps[:, 0:NODES]).then_inc(acc_done, 1)
                dve.wait_ge(acc_done, 1)

        def general_act(act):
            s = G[0]
            with act.Fori(0, GROUPS) as g:
                act.wait_ge(s["sum"], g + 1)
                nc.scalar.activation(gath[:, 0, :, :], gath[:, 0, :, :], ACT.Relu).then_inc(s["msg"], 1)

        def scale_h(act, n0, n1):
            nc.scalar.activation(hT[:, n0:n1], hT[:, n0:n1], ACT.Copy, scale=eps1p[:, 0:1]).then_inc(h_scaled, 1)

        H_CUTS = [0, UNIT] + [UNIT + (ROWS - UNIT) * k // UNROLL for k in range(1, UNROLL + 1)]

        def norms_dve(dve):
            count = [0]

            def link(ins):
                count[0] += 1
                ins.then_inc(norm_chain, 1)
                dve.wait_ge(norm_chain, count[0])

            def inverses():
                dve.wait_ge(norm_stds, 2)
                nc.vector.tensor_tensor(tmp1[:, 3, :], bm1, m1, ALU.subtract)
                nc.vector.tensor_tensor(tmp2[0:PARTS, 3, :], bm2[0:PARTS, :], m2[0:PARTS, :], ALU.subtract)
                nc.vector.tensor_tensor(brow_f[:, 1, :], bb1[0:PARTS, :], bb2[0:PARTS, :], ALU.add)
                nc.vector.reciprocal(tmp1[:, 2, :], tmp1[:, 1, :])
                link(nc.vector.reciprocal(tmp2[:, 2, :], tmp2[:, 1, :]))

            def scales():
                nc.vector.tensor_tensor(scale1[:, :], tmp1[:, 2, :], g1, ALU.mult)
                link(nc.vector.tensor_tensor(scale2, tmp2[:, 2, :], g2, ALU.mult))
                nc.vector.tensor_tensor(tmp1[:, 0, :], tmp1[:, 3, :], scale1[:, :], ALU.mult)
                link(nc.vector.tensor_tensor(tmp2[0:PARTS, 0, :], tmp2[0:PARTS, 3, :], scale2[0:PARTS, :], ALU.mult))
                nc.vector.tensor_tensor(bias1[:, :], tmp1[:, 0, :], b1, ALU.add)
                link(nc.vector.tensor_tensor(brow_f[:, 0, :], tmp2[0:PARTS, 0, :], b2[0:PARTS, :], ALU.add))

            def bias_parts():
                link(nc.vector.tensor_copy(brow_part, brow_f))
                link(nc.vector.scalar_tensor_tensor(out=brow_f, in0=brow_part, scalar=less_b[0:PARTS, 0:1],
                                                    in1=brow_f, op0=ALU.mult, op1=ALU.add))
                link(nc.vector.tensor_copy(brow_part, brow_f))
                link(nc.vector.scalar_tensor_tensor(out=brow[:, 0:2, :], in0=brow_part,
                                                    scalar=less_b[0:PARTS, 1:2], in1=brow_f,
                                                    op0=ALU.mult, op1=ALU.add))

            def second_weights():
                for h in range(HALVES):
                    ins = nc.vector.tensor_tensor(wm2[:, h, :], wm2[:, h, :], scale2, ALU.mult)
                link(ins)
                for s, n in START_UNITS.items():
                    dve.sem_inc(s, n)

            return [inverses, scales, bias_parts, second_weights]

        def node_pe(pe, unit, nb, step):
            if step == 0:
                pe.wait_ge(r_done, unit(1, 1))
                pe.wait_ge(x1T_done, unit(1, 1))
            if step in range(4):
                h, n = step // 2, nb * BLOCK // 2
                k = step % 2 * n
                nc.tensor.matmul(psZ[h][:, k:k + n], wm1[:, h * P:(h + 1) * P], hT[:, bass.ds(unit(UNIT, k), n)],
                                 start=True, stop=True).then_inc(z_done, 1)
            if step in range(5, 5 + nb):
                b = step - 5
                if b == 0:
                    pe.wait_ge(r_done, unit(1, 2))
                    pe.wait_ge(res_done, unit(1, 1))
                for h in range(HALVES):
                    nc.tensor.matmul(psY[:, b * D:(b + 1) * D], rT[:, h, b * BLOCK:(b + 1) * BLOCK],
                                     wm2[:, h, :], start=(h == 0), stop=False)
                mm = nc.tensor.matmul(psY[:, b * D:(b + 1) * D], brow[:, 2, :], brow[:, 0, :],
                                      start=False, stop=True)
                if b == nb - 1:
                    mm.then_inc(y_done, 1)
            if step == 11:
                pe.wait_ge(x1_done, unit(1, 1))
                for b in range(nb):
                    mm = nc.tensor.transpose(psT[:, b * BLOCK:(b + 1) * BLOCK], x1s[:, b, :], ident[:, :])
                mm.then_inc(xt_done, 1)
            if step in (12, 13):
                if step == 12:
                    pe.wait_ge(x1T_done, unit(1, 2))
                    pe.wait_ge(y_sb, unit(1, 1))
                for b in range(2 * (step - 12), min(2 * (step - 11), nb)):
                    nc.tensor.matmul(psY[:, b * D:(b + 1) * D], x1T[:, b * BLOCK:(b + 1) * BLOCK], w1T,
                                     start=True, stop=False)
                    mm = nc.tensor.matmul(psY[:, b * D:(b + 1) * D], brow[:, 2, :], brow[:, 1, :],
                                          start=False, stop=True)
                    if b == nb - 1:
                        mm.then_inc(o1_done, 1)

        def node_act(act, unit, nb, step):
            if step in (2, 4):
                h = step // 2 - 1
                act.wait_ge(z_done, unit(4, step))
                if h == 0:
                    act.wait_ge(o1_done, unit(1, 1))
                ins = nc.scalar.activation(rT[:, h, 0:nb * BLOCK], psZ[h][:, 0:nb * BLOCK], ACT.Relu,
                                           bias=bias1[:, h:h + 1], scale=scale1[:, h:h + 1])
                if h == 1:
                    ins.then_inc(r_done, 1)
            if step == 10:
                act.wait_ge(var_done, unit(1, 1))
                nc.scalar.activation(std[:, 0:nb], mean_var[:, 0:nb, 1], ACT.Sqrt, bias=epsc[:, 0:1])\
                    .then_inc(std_done, 1)
            if step == 11:
                act.wait_ge(x1_done, unit(1, 1))
                act.dma_start(x1_dram[bass.ds(unit(UNIT), nb * BLOCK), :].rearrange("(k p) d -> p k d", p=BLOCK),
                              x1s[:, 0:nb, :]).then_inc(x1_stored, 16)
                act.wait_ge(y_done, unit(1, 1))
                act.wait_ge(xt_done, unit(1, 2))
                nc.scalar.copy(x1T[:, 0:nb * BLOCK], psT[:, 0:nb * BLOCK]).then_inc(x1T_done, 1)
            if step == 14:
                act.wait_ge(res_done, unit(1, 2))
                act.dma_start(res_dram[bass.ds(unit(UNIT), nb * BLOCK), :].rearrange("(k p) d -> p k d", p=BLOCK),
                              x_in[:, 0:nb, :]).then_inc(res_stored, 16)

        def node_dve(dve, unit, nb, step):
            if step == 9:
                dve.wait_ge(x_loaded, unit(16, 16))
                dve.wait_ge(y_done, unit(1, 1))
                nc.vector.tensor_tensor(x_in[:, 0:nb, :], x_in[:, 0:nb, :],
                                        psY[:, 0:nb * D].rearrange("p (k d) -> p k d", d=D), ALU.add)\
                    .then_inc(y_sb, 1)
                dve.wait_ge(y_sb, unit(1, 1))
                for b in range(nb):
                    ins = nc.vector.bn_stats(stats[:, b, :], x_in[:, b, :])
                ins.then_inc(stats_done, 1)
                dve.wait_ge(stats_done, unit(1, 1))
                dve.wait_ge(std_done, unit(1, 1))
                dve.sem_inc(dve_step, 1)
                for b in range(nb):
                    ins = nc.vector.bn_aggr(mean_var[:, b, :], stats[:, b, :])
                ins.then_inc(var_done, 1)
            if step == 10:
                dve.wait_ge(std_done, unit(1, 2))
                nc.vector.reciprocal(rstd[:, 0:nb], std[:, 0:nb]).then_inc(rstd_done, 1)
                dve.wait_ge(rstd_done, unit(1, 1))
                dve.wait_ge(x1_stored, unit(16, 16))
                dve.wait_ge(xt_done, unit(1, 1))
                for b in range(nb):
                    ins = nc.vector.tensor_scalar(x1s[:, b, :], x_in[:, b, :], mean_var[:, b, 0:1],
                                                  rstd[:, b:b + 1], ALU.subtract, ALU.mult)
                ins.then_inc(x1_done, 1)
            if step == 14:
                dve.wait_ge(o1_done, unit(1, 2))
                dve.wait_ge(x1_done, unit(1, 1))
                nc.vector.tensor_tensor(x_in[:, 0:nb, :], x1s[:, 0:nb, :],
                                        psY[:, 0:nb * D].rearrange("p (k d) -> p k d", d=D), ALU.add)\
                    .then_inc(res_done, 1)

        def node_sp(sp, unit, nb):
            sp.wait_ge(res_stored, unit(16, 16))
            sp.dma_start(x_in[:, 0:nb, :],
                         x[bass.ds(unit(UNIT), nb * BLOCK), :].rearrange("(k p) d -> p k d", p=BLOCK))\
                .then_inc(x_loaded, 16)

        def node_steps(eng, node, m, steps=range(STEPS)):
            for step in steps:
                node(eng, linear(m), unit_blocks(m), step)

        def turns(eng, turn_of, behind_first=None):
            for t0, t1, units in segments():
                if units is None:
                    if t1 - t0 == 1:
                        turn_of(linear(t0), None, 0, 'first' if t0 == 0 else None)
                    else:
                        with eng.Fori(t0, t1) as i:
                            turn_of(linear(i), None, 0, None)
                    if t0 == 0 and behind_first is not None:
                        behind_first(eng)
                    continue
                m0, m1 = units

                def turns_of_unit(m):
                    for part in range(SPAN):
                        last = m1 - m0 == 1 and t0 + part == TURNS - 1
                        turn_of(linear(m, SPAN, t0 - SPAN * m0 + part), linear(m), part, "last" if last else None)

                if m1 - m0 == 1:
                    turns_of_unit(m0)
                else:
                    with eng.Fori(m0, m1) as m:
                        turns_of_unit(m)

        NB = UNIT // BLOCK

        def efd_load(sp, at, k):
            sp.dma_start(ef_d[:, k, :], efT[:, bass.ds(at, PEDGES)].rearrange("r (s c) -> r s c", s=SEGS))\
                .then_inc(efd_in[k], 16)

        def ef_split_hi(act, loaded, used, k):
            act.wait_ge(efd_in[k], loaded)
            if used is not None:
                act.wait_ge(ef_in[k], used)
            nc.scalar.copy(ef_p[:, k, 0, :], ef_d[:, k, :]).then_inc(ef_hi, 1)

        def ef_split_rest(dve, h, k):
            dve.wait_ge(ef_hi, h + 1)
            nc.vector.tensor_tensor(ef_d[:, k, :], ef_d[:, k, :], ef_p[:, k, 0, :], ALU.subtract)\
                .then_inc(ef_rest, 1)

        def ef_split_mid(act, h, k):
            act.wait_ge(ef_rest, h + 1)
            nc.scalar.copy(ef_p[:, k, 1, :], ef_d[:, k, :]).then_inc(ef_mid, 1)

        def ef_split_lo(dve, h, k):
            dve.wait_ge(ef_mid, h + 1)
            nc.vector.tensor_tensor(ef_p[:, k, 2, :], ef_d[:, k, :], ef_p[:, k, 1, :], ALU.subtract)\
                .then_inc(ef_lo, 1)

        def ef_stack(sp, h, k):
            sp.wait_ge(ef_lo, h + 1)
            for row, part in enumerate(FEATURE_PARTS):
                sp.dma_start(ef[row * EF:(row + 1) * EF, k, :].rearrange("r (s c) -> r s c", s=SEGS),
                             ef_p[:, k, part, :]).then_inc(ef_in[k], 16)

        def load_idx(sp, turn, u):
            sp.dma_start(idx[:, u, :], src_t[:, bass.ds(turn(UNROLL * GROUP, u * GROUP), GROUP)])\
                .then_inc(idx_in[u], 16)

        def gather(pool, u):
            for j in range(GROUP):
                pool.indirect_dma_start(gath[:, u, j, :], None, x, bass.IndirectOffsetOnAxis(idx[:, u, j:j + 1], 0))\
                    .then_inc(gathered[u], 16)

        def edges_sp(sp):
            def turn_of(turn, unit, part, end):
                if unit is not None and part == 1:
                    node_sp(sp, unit, NB)
                for k in range(UNROLL // 2):
                    if end != "first":
                        for u in (2 * k, 2 * k + 1):
                            sp.wait_ge(sum_done, turn(UNROLL, u + 1))
                            load_idx(sp, turn, u)
                        ef_stack(sp, turn(2, k), k)
                    if end != "last":
                        if end == "first":
                            sp.wait_ge(ef_lo, k + 1)
                        efd_load(sp, turn(2 * PEDGES, (2 + k) * PEDGES), k)

            turns(sp, turn_of)

        def edges_pool(pool):
            with pool.Fori(1, TURNS) as i:
                for u in range(UNROLL):
                    pool.wait_ge(idx_in[u], i * 16 + 16)
                    pool.wait_ge(p_done, i * UNROLL + (u + 1))
                    pool.sem_inc(pool_step, 1)
                    gather(pool, u)

        def edges_pe(pe):
            def features(turn, u):
                k, e0 = u // 2, u % 2 * GEDGES
                if u % 2 == 0:
                    pe.wait_ge(ef_in[k], turn(16 * len(FEATURE_PARTS), 16 * len(FEATURE_PARTS)))
                pe.wait_ge(sum_done, turn(UNROLL, u + 4))
                for j in range(GROUP):
                    mm = nc.tensor.matmul(psE[:, j * D:(j + 1) * D], ef[0:STACK, k, e0 + j * P:e0 + (j + 1) * P],
                                          wc[:, :], start=True, stop=True)
                mm.then_inc(e_done, 1)

            def sums_before(turn, u):
                v = (u - 1) % UNROLL
                pe.wait_ge(od_done, turn(UNROLL, u))
                pe.wait_ge(added, turn(UNROLL, u))
                pe.wait_ge(msg_done, turn(UNROLL, u))
                for j in range(GROUP):
                    mm = nc.tensor.matmul(psP[v % 2], gath[:, v, j, :], od[:, v % 2, j, :],
                                          start=(j == 0), stop=(j == GROUP - 1))
                mm.then_inc(p_done, 1)

            def counts(turn, u, of):
                own = [ob[:, u % 2, j, :] for j in range(GROUP - 1)] + [ob_last[:, u, :]]
                before = [ob_last[:, (u - 1) % UNROLL, :]] + own[:-1]
                if of[0] == 0:
                    pe.wait_ge(ob_done, turn(UNROLL, u + 1))
                    pe.wait_ge(mvc_done, turn(UNROLL, u + 1))
                for j in of:
                    tile = turn(UNROLL * GROUP, u * GROUP + j + 1)
                    pe.wait_ge(copied, tile)
                    pe.wait_ge(mv_done, tile)
                    nc.tensor.matmul(psA[j % 2], own[j], mv[:, j, :], start=True, stop=False,
                                     skip_group_check=True).then_inc(mv_used, 1)
                    nc.tensor.matmul(psA[j % 2].rearrange("p (a w) -> p a w", w=CWIN)[:, :, 0], before[j],
                                     mvc[:, u % 2, j, :], start=False, stop=True, skip_group_check=True)\
                        .then_inc(a_done, 1)

            def turn_of(turn, unit, part, end):
                for u in range(UNROLL):
                    counts(turn, u, (0, 1))
                    if not (end == "first" and u == 0):
                        sums_before(turn, u)
                    counts(turn, u, (2, 3))
                    if u + 1 < UNROLL:
                        features(turn, u + 1)
                    elif end != "last":
                        features(lambda k, c: turn(k, k + c), 0)
                    step = part * UNROLL + u - 1
                    if unit is not None and step >= 0:
                        if step == 0:
                            pe.wait_ge(added, turn(UNROLL, 2))
                        node_pe(pe, unit, NB, step)

            features(linear(0), 0)
            turns(pe, turn_of)
            sums_before(linear(TURNS), 0)

        def load_bases(eng, at, n):
            return nc.values_load_multi_w_load_instructions(
                bases[0:1, bass.ds(at, n)], engines=[eng.engine], min_val=0, max_val=NODES - 1,
                skip_runtime_bounds_check_because="they are destinations, which are nodes")[1]

        def edges_dve(dve):
            def one_hots(turn, u):
                k, tiles = u % 2, turn(UNROLL * GROUP, u * GROUP)
                dve.wait_ge(a_done, turn(UNROLL * GROUP, (u + 1) * GROUP))
                for j in range(GROUP):
                    own = ob[:, k, j, :] if j < GROUP - 1 else ob_last[:, u, :]
                    ins = nc.vector.tensor_scalar(own, iota[:, 0:BLOCK],
                                                  b_key[:, bass.ds(turn(UNROLL * GROUP, u * GROUP + j), 1)], None,
                                                  ALU.is_equal)
                ins.then_inc(ob_done, 1)
                nc.vector.tensor_tensor(mvc[:, k, :, :],
                                        iota[:, 0:BLOCKS].unsqueeze(1).to_broadcast([P, GROUP, BLOCKS]),
                                        c_key[:, bass.ds(tiles, GROUP)].unsqueeze(2).to_broadcast([P, GROUP, BLOCKS]),
                                        ALU.is_equal).then_inc(mvc_done, 1)
                for j in range(GROUP):
                    dve.wait_ge(mv_used, turn(UNROLL * GROUP, u * GROUP + j + 1))
                    nc.vector.tensor_scalar(mv[:, j, :], iota[:, 0:CCOLS],
                                            m_key[:, bass.ds(turn(UNROLL * GROUP, u * GROUP + j), 1)],
                                            None, ALU.is_equal).then_inc(mv_done, 1)

            def windows(turn, u):
                dve.wait_ge(p_done, turn(UNROLL, u + 3))
                nc.vector.tensor_tensor(od[:, u % 2, :, :],
                                        iota[:, 0:WIN].unsqueeze(1).to_broadcast([P, GROUP, WIN]),
                                        d_key[:, bass.ds(turn(UNROLL * GROUP, u * GROUP), GROUP)].unsqueeze(2)
                                        .to_broadcast([P, GROUP, WIN]), ALU.is_equal).then_inc(od_done, 1)

            def add_before(turn, u):
                base, = load_bases(dve, turn(UNROLL * GROUP, (u - 1) * GROUP), 1)
                dve.wait_ge(p_done, turn(UNROLL, u + 4))
                dve.wait_ge(added, turn(UNROLL, u + 1))
                to = hT[:, bass.ds(base, WIN)]
                nc.vector.tensor_tensor(to, psP[(u - 1) % 2], to, ALU.add).then_inc(added, 1)

            def turn_of(turn, unit, part, end):
                for u in range(UNROLL):
                    dve.wait_ge(e_done, turn(UNROLL, u + 3))
                    dve.wait_ge(gathered[u], turn(16 * GROUP, 16 * GROUP))
                    nc.vector.tensor_tensor(gath[:, u, :, :], psE.rearrange("p (j d) -> p j d", j=GROUP),
                                            gath[:, u, :, :], ALU.add).then_inc(sum_done, 1)
                    following, v = (turn, u + 1) if u + 1 < UNROLL else (lambda k, c=0: turn(k, k + c), 0)
                    more = not (end == "last" and u == UNROLL - 1)
                    if more:
                        one_hots(following, v)
                    if not (end == "first" and u == 0):
                        add_before(turn, u)
                    if more:
                        windows(following, v)
                    if end != "last":
                        (ef_split_lo if u % 2 else ef_split_rest)(dve, turn(2, u // 2 + 2), u // 2)
                    if end == "first":
                        pieces[u]()
                    if unit is not None:
                        node_dve(dve, unit, NB, part * UNROLL + u - 1)

            pieces = norms_dve(dve)
            one_hots(linear(0), 0)
            windows(linear(0), 0)
            dve.wait_ge(h_scaled, 1)
            turns(dve, turn_of, lambda dve: dve.wait_ge(h_scaled, len(H_CUTS) - 1))
            add_before(linear(TURNS), 0)

        def edges_act(act):
            def copy_counts(turn, u, of, base):
                for j in of:
                    act.wait_ge(a_done, turn(UNROLL * GROUP, u * GROUP + j + 9))
                    act.wait_ge(copied, turn(UNROLL * GROUP, u * GROUP + j + 2))
                    nc.scalar.copy(AT[:, :, bass.ds(base[j], CWIN)],
                                   psA[j % 2].rearrange("p (a w) -> p a w", w=CWIN)).then_inc(copied, 1)

            def turn_of(turn, unit, part, end):
                for u in range(UNROLL):
                    base = load_bases(act, turn(UNROLL * GROUP, u * GROUP), GROUP)
                    copy_counts(turn, u, (0, 1), base)
                    act.wait_ge(sum_done, turn(UNROLL, u + 5))
                    nc.scalar.activation(gath[:, u, :, :], gath[:, u, :, :], ACT.Relu).then_inc(msg_done, 1)
                    if end != "last" and u % 2 == 0:
                        ef_split_hi(act, turn(16, 32), turn(16 * len(FEATURE_PARTS), 16 * len(FEATURE_PARTS)), u // 2)
                    if end != "last" and u % 2:
                        ef_split_mid(act, turn(2, u // 2 + 2), u // 2)
                    copy_counts(turn, u, (2, 3), base)
                    if end == "first":
                        scale_h(act, H_CUTS[u + 1], H_CUTS[u + 2])
                    if unit is not None:
                        node_act(act, unit, NB, part * UNROLL + u - 1)

            turns(act, turn_of)

        def part(q, k):
            return x1p(q)[:, k, :, :]

        def flat(a, q):
            return a[:, 0:unit_blocks(q) * D].rearrange("p (b d) -> p b d", d=D)

        def split_sp(sp, q):
            if q >= 2:
                sp.wait_ge(rest_done, q - 1)
            sp.wait_ge(x1_stored, 16 * (q + 2))
            sp.dma_start(flat(xr[q % 2], q), x1_dram[q * UNIT:q * UNIT + unit_blocks(q) * BLOCK, :]
                         .rearrange("(k p) d -> p k d", p=BLOCK)).then_inc(xr_in[q % 2], 16)

        def split_hi(act, q):
            act.wait_ge(xr_in[q % 2], 16 * (q // 2 + 1))
            nc.scalar.copy(part(q, 0), flat(xr[q % 2], q)).then_inc(hi_done, 1)

        def split_mid(act, q):
            act.wait_ge(rest_done, q + 1)
            nc.scalar.copy(part(q, 1), flat(rest, q)).then_inc(mid_done, 1)

        def split_dve(dve, q):
            dve.wait_ge(hi_done, q + 1)
            if q:
                dve.wait_ge(lo_done, q)
            nc.vector.tensor_tensor(flat(rest, q), flat(xr[q % 2], q), part(q, 0), ALU.subtract)\
                .then_inc(rest_done, 1)
            dve.wait_ge(mid_done, q + 1)
            nc.vector.tensor_tensor(part(q, 2), flat(rest, q), part(q, 1), ALU.subtract).then_inc(lo_done, 1)

        def gather_unit(pe, c, q):
            n0, n1 = chunks[c]
            pe.wait_ge(lo_done, q + 1)
            for b in range(q * (UNIT // BLOCK), q * (UNIT // BLOCK) + unit_blocks(q)):
                for k in range(PARTS):
                    mm = nc.tensor.matmul(psAcc[c % len(psAcc)][:, 0:n1 - n0], x1p(q)[:, k, b % (UNIT // BLOCK), :],
                                          AT[:, b, n0:n1],
                                          start=(b == 0 and k == 0), stop=(b == BLOCKS - 1 and k == PARTS - 1))
            if q == UNITS - 1:
                mm.then_inc(acc_done, 1)

        def output_pe(pe, c):
            n0, n1 = chunks[c]
            pe.wait_ge(agg_done, c + 1)
            if c >= 2:
                pe.wait_ge(f_sb, c - 1)
            for b in range((n1 - n0) // OROWS):
                mm = nc.tensor.matmul(psO[c % 2][0:OROWS, b * D:(b + 1) * D],
                                      aggT[:, c % 2, b * OROWS:(b + 1) * OROWS], w2T, start=True, stop=True)
            mm.then_inc(o_done, 1)

        res = [x_in, flat(xr[0], 0)]
        fin = [x1s, flat(xr[1], 0)]

        def output_load(sp, c):
            n0, n1 = chunks[c]
            if c >= 2:
                sp.wait_ge(fin_done, c - 1)
            sp.dma_start(res[c % 2][0:OROWS, 0:(n1 - n0) // OROWS, :], res_dram[n0:n1, :]
                         .rearrange("(k p) d -> p k d", p=OROWS)).then_inc(res_in[c % 2], 16)

        def output_store(sp, c):
            n0, n1 = chunks[c]
            m, k = OROWS, (n1 - n0) // OROWS
            sp.wait_ge(fin_done, c + 1)
            sp.dma_start(out[n0:n1, :].rearrange("(k p) d -> p k d", p=m), fin[c % 2][0:m, 0:k, :])\
                .then_inc(stored[c % 2], 16)

        def output_dve(dve, c):
            n0, n1 = chunks[c]
            m, k = OROWS, (n1 - n0) // OROWS
            r, f = res[c % 2], fin[c % 2]
            dve.wait_ge(o_done, c + 1)
            dve.wait_ge(res_in[c % 2], 16 * (c // 2 + 1))
            nc.vector.tensor_tensor(r[0:m, 0:k, :], r[0:m, 0:k, :],
                                    psO[c % 2][0:m, 0:k * D].rearrange("p (k d) -> p k d", d=D), ALU.add)\
                .then_inc(f_sb, 1)
            dve.wait_ge(f_sb, c + 1)
            for b in range(k):
                ins = nc.vector.bn_stats(stats[0:m, b, :], r[0:m, b, :])
            ins.then_inc(f_stats, 1)
            dve.wait_ge(f_stats, c + 1)
            if c:
                dve.wait_ge(f_std, c)
            for b in range(k):
                ins = nc.vector.bn_aggr(mean_var[0:m, b, :], stats[0:m, b, :])
            ins.then_inc(f_var, 1)
            dve.wait_ge(f_std, c + 1)
            nc.vector.reciprocal(rstd[0:m, 0:k], std[0:m, 0:k]).then_inc(f_rstd, 1)
            dve.wait_ge(f_rstd, c + 1)
            if c >= 2:
                dve.wait_ge(stored[c % 2], 16 * (c // 2))
            for b in range(k):
                ins = nc.vector.tensor_scalar(f[0:m, b, :], r[0:m, b, :], mean_var[0:m, b, 0:1],
                                              rstd[0:m, b:b + 1], ALU.subtract, ALU.mult)
            ins.then_inc(fin_done, 1)

        def output_act(act, c, sums):
            n0, n1 = chunks[c]
            m, k = OROWS, (n1 - n0) // OROWS
            if c >= 2:
                act.wait_ge(o_done, c - 1)
            nc.scalar.copy(aggT[:, c % 2, 0:n1 - n0], sums).then_inc(agg_done, 1)
            act.wait_ge(f_var, c + 1)
            nc.scalar.activation(std[0:m, 0:k], mean_var[0:m, 0:k, 1], ACT.Sqrt, bias=epsc[0:m, 0:1])\
                .then_inc(f_std, 1)

        def the_flag(eng):
            eng.wait_ge(flag_done, 1)
            return eng.value_load(flag[0:1, 0:1], min_val=0, max_val=1 << 20)

        AHEAD = len(psAcc)
        A, B = LATE

        @block.sync
        def _(sp):
            sp.dma_start(idx[:, :, :], src_t[:, 0:UNROLL * GROUP].rearrange("p (u j) -> p u j", j=GROUP))\
                .then_inc(idx_in[0], 16)
            for to, of in ((rw, rows[:, 0:8 * D].to_broadcast([P, 8 * D])), (wt, wtmp),
                           (eps1p[:, :], rows[:, 8 * D:].to_broadcast([P, 1]))):
                sp.dma_start(to, of).then_inc(weights, 16)
            for to, of in ((dst_ai, dst_a), (dst_bi, dst_b), (spans_t, spans)):
                sp.dma_start(to, of).then_inc(flag_loads, 16)
            for h in range(2):
                efd_load(sp, h * PEDGES, h)
            for to, of in ((src_i, src_t), (dst_i, dst_t), (base_t, first.to_broadcast([P, TILES])),
                           (bases[:, :], first)):
                sp.dma_start(to, of).then_inc(key_loads, 16)
            sp.dma_start(hT[:, 0:ROWS], xT).then_inc(h_loaded, 16)
            sp.dma_start(wf[:, :], wfix).then_inc(loads, 16)
            for h in range(2):
                ef_stack(sp, h, h)
            f = the_flag(sp)
            with sp.If(f > 0):
                general_sp(sp, 0)
                for m in range(UNITS):
                    node_sp(sp, linear(m), unit_blocks(m))
                sp.wait_ge(x1_stored, 16 * UNITS + 16)
                general_sp(sp, 1)
                sp.wait_ge(agg_done, 1)
            with sp.Else():
                edges_sp(sp)
                sp.wait_ge(e_done, GROUPS + 2)
                for q in range(2):
                    split_sp(sp, q)
                node_sp(sp, linear(A), unit_blocks(A))
                for q in range(2, 4):
                    split_sp(sp, q)
                node_sp(sp, linear(B), unit_blocks(B))
                for q in (4, A, B):
                    split_sp(sp, q)
                sp.wait_ge(lo_done, UNITS)
            sp.wait_ge(res_stored, 16 * UNITS + 16)
            for c in range(len(chunks)):
                output_load(sp, c)
                if c:
                    output_store(sp, c - 1)
            output_store(sp, len(chunks) - 1)
            for k in range(2):
                sp.wait_ge(stored[k], 16 * len(chunks[k::2]))

        @block.gpsimd
        def _(pool):
            nc.gpsimd.iota(iota[:, 0:CCOLS], [[1, CCOLS]], base=0, channel_multiplier=0,
                           allow_small_or_imprecise_dtypes=True).then_inc(pool_consts, 1)
            nc.gpsimd.memset(ident[:, :], 0.0).then_inc(pool_consts, 1)
            pool.wait_ge(pool_consts, 2)
            nc.gpsimd.affine_select(out=ident[:, :], in_=ident[:, :], compare_op=ALU.not_equal, fill=1.0, base=0,
                                    pattern=[[-1, P]], channel_multiplier=1).then_inc(pool_consts, 1)
            pool.wait_ge(idx_in[0], 16)
            pool.sem_inc(pool_step, 1)
            for u in range(UNROLL):
                gather(pool, u)
            f = the_flag(pool)
            with pool.If(f > 0):
                general_pool(pool, 0)
                pool.wait_ge(x1_stored, 16 * UNITS + 16)
                general_pool(pool, 1)
            with pool.Else():
                edges_pool(pool)
            pool.wait_ge(x1_stored, 16 * UNITS + 16)

        @block.scalar
        def _(act):
            act.wait_ge(consts, 1)
            act.wait_ge(weights, 16 * 3)
            nc.scalar.activation(tmp2[:, 1, :], v2, ACT.Sqrt, bias=epsb[:, 0:1]).then_inc(norm_stds, 1)
            for h in range(2):
                ef_split_hi(act, 16, None, h)
            for h in range(2):
                ef_split_mid(act, h, h)
            act.wait_ge(h_loaded, 16)
            act.wait_ge(eps_done, 1)
            scale_h(act, 0, UNIT)
            act.wait_ge(loads, 16)
            nc.scalar.activation(tmp1[:, 1, :], v1, ACT.Sqrt, bias=epsb[:, 0:1]).then_inc(norm_stds, 1)
            act.wait_ge(keys_done, 1)
            f = the_flag(act)
            with act.If(f > 0):
                for n0, n1 in zip(H_CUTS[1:], H_CUTS[2:]):
                    scale_h(act, n0, n1)
                general_act(act)
                for m in range(UNITS):
                    node_steps(act, node_act, m)
                act.wait_ge(acc_done, 1)
                for c, (n0, n1) in enumerate(chunks):
                    output_act(act, c, hot[:, n0:n1])
            with act.Else():
                edges_act(act)
                act.wait_ge(p_done, GROUPS + 4)
                act.wait_ge(a_done, TILES + 8)
                split_hi(act, 0)
                node_steps(act, node_act, A, (2, 4))
                split_mid(act, 0)
                split_hi(act, 1)
                split_mid(act, 1)
                node_steps(act, node_act, A, (10, 11))
                split_hi(act, 2)
                split_mid(act, 2)
                node_steps(act, node_act, A, (14,))
                node_steps(act, node_act, B, (2, 4))
                split_hi(act, 3)
                split_mid(act, 3)
                node_steps(act, node_act, B, (10, 11))
                split_hi(act, 4)
                split_mid(act, 4)
                node_steps(act, node_act, B, (14,))
                for q in (A, B):
                    split_hi(act, q)
                    split_mid(act, q)
                for c, (n0, n1) in enumerate(chunks):
                    act.wait_ge(acc_done, c + 1)
                    output_act(act, c, psAcc[c % AHEAD][:, 0:n1 - n0])
            act.wait_ge(x1_stored, 16 * UNITS + 16)
            act.wait_ge(res_stored, 16 * UNITS + 16)

        @block.vector
        def _(dve):
            count = [0]

            def link(ins):
                count[0] += 1
                ins.then_inc(vchain, 1)
                dve.wait_ge(vchain, count[0])

            for s, n in START.items():
                dve.sem_inc(s, n)
            nc.vector.memset(ones[:, :], 1.0)
            nc.vector.memset(viol[:, :], 0.0)
            nc.vector.memset(ob_last[:, UNROLL - 1, :], 0.0)
            nc.vector.memset(hT[:, ROWS:], 0.0)
            nc.vector.memset(brow[:, 2, :], 1.0)
            nc.vector.memset(unit_row[:, 0:ONES_AT], 0.0)
            nc.vector.memset(unit_row[:, ONES_AT:STACK], 1.0)
            nc.vector.memset(c_key[:, 0:1], -1.0)
            nc.vector.memset(epsc[:, :], LN_EPS)
            nc.vector.memset(epsb[:, :], BN_EPS)
            nc.vector.memset(ef[ONES_AT:STACK, :, :], 1.0)
            link(nc.vector.memset(chk, 0.0))
            dve.sem_inc(consts, 1)
            dve.wait_ge(weights, 16 * 3)
            nc.vector.tensor_scalar(eps1p[:, :], eps1p[:, :], 1.0, None, ALU.add).then_inc(eps_done, 1)
            dve.wait_ge(flag_loads, 16 * 3)
            tf, tl, next1, next2 = [spans_t[:, k * GROUP:(k + 1) * GROUP] for k in range(4)]
            nc.vector.tensor_tensor(t_f, dst_ai, dst_bi, ALU.is_gt)
            nc.vector.tensor_tensor(diffs[:, 0:GROUP], tl, tf, ALU.subtract)
            nc.vector.tensor_tensor(diffs[:, 2 * GROUP:], tl[:, GROUP - 1:], tf[:, 0:1], ALU.subtract)
            nc.vector.tensor_tensor(diffs[:, GROUP:2 * GROUP], next1, tf, ALU.subtract)
            nc.vector.tensor_tensor(chk[:, 0:GROUP], tl, next2, ALU.is_ge)
            nc.vector.tensor_scalar(chk[0:1, GROUP:GROUP + 1], tf[0:1, 0:1], 0.0, None, ALU.not_equal)
            link(nc.vector.tensor_tensor(chk[:, GROUP + 1:GROUP + 2], spans_t[:, 4 * GROUP:4 * GROUP + 1],
                                         spans_t[:, 4 * GROUP + 1:], ALU.is_lt))
            nc.vector.tensor_reduce(viol[:, 1:2], t_f, AX_X, ALU.add)
            nc.vector.tensor_scalar(chk[:, GROUP + 2:2 * GROUP + 2], diffs[:, 0:GROUP], float(CWIN - 1), None,
                                    ALU.is_gt)
            nc.vector.tensor_scalar(chk[:, 2 * GROUP + 2:2 * GROUP + 3], diffs[:, 2 * GROUP:], float(WIN - 1), None,
                                    ALU.is_gt)
            link(nc.vector.tensor_scalar(chk[:, 2 * GROUP + 3:], diffs[:, GROUP:2 * GROUP], float(CWIN), None,
                                         ALU.is_gt))
            link(nc.vector.tensor_reduce(viol[0:GROUPS, 0:1], chk, AX_X, ALU.add))
            nc.vector.tensor_reduce(t_f[:, 0:1], viol[:, :], AX_X, ALU.add).then_inc(viol_done, 1)
            for h in range(2):
                ef_split_rest(dve, h, h)
            for h in range(2):
                ef_split_lo(dve, h, h)
            dve.wait_ge(viol_sum, 1)
            nc.vector.tensor_copy(flag[:, :], psY[0:1, 0:1]).then_inc(flag_done, 1)
            dve.wait_ge(key_loads, 16 * 4)
            nc.vector.tensor_scalar(t_i, src_i, 7, None, ALU.logical_shift_right)
            link(nc.vector.tensor_tensor(t_f, dst_i, base_t, ALU.subtract))
            nc.vector.tensor_copy(a_f, t_i)
            by_tile = base_t.rearrange("p (g j) -> p g j", j=GROUP)
            link(nc.vector.tensor_tensor(d_key.rearrange("p (g j) -> p g j", j=GROUP),
                                         dst_i.rearrange("p (g j) -> p g j", j=GROUP),
                                         by_tile[:, :, 0:1].to_broadcast([P, GROUPS, GROUP]), ALU.subtract))
            nc.vector.scalar_tensor_tensor(out=m_key, in0=a_f, scalar=float(CWIN), in1=t_f,
                                           op0=ALU.mult, op1=ALU.add)
            link(nc.vector.tensor_scalar(t_i, src_i, BLOCK - 1, None, ALU.bitwise_and))
            nc.vector.tensor_tensor(t_f[:, 1:TILES], dst_i[:, 0:TILES - 1], base_t[:, 1:TILES], ALU.not_equal)
            link(nc.vector.tensor_copy(b_key, t_i))
            dve.wait_ge(wc_done, 1)
            link(nc.vector.tensor_copy(wc_part, psE[0:STACK, 0:D]))
            nc.vector.scalar_tensor_tensor(out=c_key[:, 1:TILES], in0=t_f[:, 1:TILES], scalar=NO_BLOCK,
                                           in1=a_f[:, 0:TILES - 1], op0=ALU.mult, op1=ALU.add)
            link(nc.vector.scalar_tensor_tensor(out=wc_rest, in0=wc_part, scalar=less[0:STACK, 0:1],
                                                in1=psE[0:STACK, 0:D], op0=ALU.mult, op1=ALU.add))
            link(nc.vector.tensor_copy(wc_part, wc_rest))
            link(nc.vector.scalar_tensor_tensor(out=wc[:, :], in0=wc_part, scalar=less[0:STACK, 1:2],
                                                in1=wc_rest, op0=ALU.mult, op1=ALU.add))
            dve.wait_ge(pool_consts, 3)
            dve.sem_inc(keys_done, 1)
            f = the_flag(dve)
            with dve.If(f > 0):
                for piece in norms_dve(dve):
                    piece()
                general_dve(dve, 0)
                for m in range(UNITS):
                    node_steps(dve, node_dve, m)
                dve.wait_ge(res_stored, 16 * UNITS + 16)
                general_dve(dve, 1)
            with dve.Else():
                edges_dve(dve)
                for q in (0, 1):
                    split_dve(dve, q)
                node_steps(dve, node_dve, A, (9, 10))
                split_dve(dve, 2)
                node_steps(dve, node_dve, A, (14,))
                split_dve(dve, 3)
                node_steps(dve, node_dve, B)
                for q in (4, A, B):
                    split_dve(dve, q)
            for c in range(len(chunks)):
                output_dve(dve, c)
            dve.wait_ge(fin_done, len(chunks))

        @block.tensor
        def _(pe):
            pe.wait_ge(viol_done, 1)
            nc.tensor.matmul(psY[0:1, 0:1], t_f[:, 0:1], ones[:, :], start=True, stop=True).then_inc(viol_sum, 1)
            pe.wait_ge(weights, 16 * 3)
            for h in range(HALVES):
                nc.tensor.matmul(psE[0:STACK, 0:D], we1T[:, h, :], we2[:, h, :], start=(h == 0), stop=False)
            nc.tensor.matmul(psE[0:STACK, 0:D], unit_row, be2[0:1, :], start=False, stop=True).then_inc(wc_done, 1)
            pe.wait_ge(keys_done, 1)
            f = the_flag(pe)
            with pe.If(f > 0):
                general_pe(pe, 0)
                pe.wait_ge(added_all, 1)
                for m in range(UNITS):
                    node_steps(pe, node_pe, m)
                general_pe(pe, 1)
                for c in range(len(chunks)):
                    output_pe(pe, c)
            with pe.Else():
                edges_pe(pe)
                pe.wait_ge(added, GROUPS + 2)
                pe.wait_ge(copied, TILES + 2)
                node_steps(pe, node_pe, A, range(9))
                gather_unit(pe, 0, 0)
                gather_unit(pe, 1, 0)
                node_steps(pe, node_pe, A, (11,))
                gather_unit(pe, 2, 0)
                node_steps(pe, node_pe, A, (12, 13))
                node_steps(pe, node_pe, B, range(4))
                gather_unit(pe, 3, 0)
                node_steps(pe, node_pe, B, (5,))
                gather_unit(pe, 0, 1)
                gather_unit(pe, 1, 1)
                node_steps(pe, node_pe, B, (11,))
                gather_unit(pe, 2, 1)
                node_steps(pe, node_pe, B, (12,))
                gather_unit(pe, 3, 1)
                for q in range(2, A):
                    for c in range(AHEAD):
                        gather_unit(pe, c, q)
                for c in range(len(chunks)):
                    if c >= AHEAD:
                        pe.wait_ge(agg_done, c - AHEAD + 1)
                    units = list(range(UNITS)) if c >= AHEAD else [A, B]
                    for q in units:
                        gather_unit(pe, c, q)
                        if c and q == units[0]:
                            output_pe(pe, c - 1)
                output_pe(pe, len(chunks) - 1)
            pe.wait_ge(fin_done, len(chunks))


def kernel(x, src, dst, edge_attr_16, L0_gnn_We1, L0_gnn_be1, L0_gnn_We2, L0_gnn_be2, L0_gnn_eps, L0_gnn_Wm1,
           L0_gnn_bm1, L0_gnn_g1, L0_gnn_b1, L0_gnn_m1, L0_gnn_v1, L0_gnn_Wm2, L0_gnn_bm2, L0_gnn_g2, L0_gnn_b2,
           L0_gnn_m2, L0_gnn_v2, L1_gnn_W1, L1_gnn_b1, L1_gnn_W2, L1_gnn_b2):
    import numpy as np
    import concourse.bacc as bacc
    from concourse.bass_utils import run_bass_kernel_spmd

    def filled(a, rows, value):
        a = np.asarray(a)
        return np.concatenate([a, np.full((rows - len(a), *a.shape[1:]), value, a.dtype)])

    def tiles(a):
        return np.ascontiguousarray(a.reshape(TILES, P).T)

    def halves(a):
        a = np.asarray(a)
        return a.reshape(HALVES, P, -1).transpose(1, 0, 2).reshape(P, -1)

    def row(a):
        return np.ascontiguousarray(np.asarray(a).reshape(1, -1))

    def less_than(part):
        return np.where(part[:, None] > np.arange(2), -1, 0).astype(np.float32)

    n = TILES * P
    src_p, dst_p, x_p = filled(src, n, 0), filled(dst, n + 1, NODES), filled(x, ROWS, 0)
    part_of = np.concatenate([np.repeat(WEIGHT_PARTS, EF), np.arange(PARTS), np.zeros(P - STACK)])
    first_p = dst_p[0:n:P]
    limits = np.zeros((GROUPS, 1), np.int32)
    starts = np.zeros((GROUPS, 1), np.int32)
    for m, t in UNIT_TURN.items():
        limits[m], starts[m] = (m + 1) * UNIT, first_p[t * UNROLL * GROUP]
    spans = [first_p, dst_p[P - 1:n:P], filled(first_p[1:], TILES, NODES), filled(first_p[2:], TILES, NODES + 1)]
    data = {
        "x": x_p, "xT": np.ascontiguousarray(x_p.T), "src_t": tiles(src_p), "dst_t": tiles(dst_p[:n]),
        "dst_a": dst_p[:n].reshape(P, TILES), "dst_b": dst_p[1:].reshape(P, TILES),
        "first": row(first_p),
        "spans": np.concatenate([a.reshape(GROUPS, GROUP) for a in spans] + [starts, limits], axis=1),
        "efT": np.ascontiguousarray(filled(edge_attr_16, n, 0).T),
        "wfix": np.concatenate([np.asarray(L0_gnn_Wm1), halves(L0_gnn_Wm2), np.asarray(L1_gnn_W1).T,
                                np.asarray(L1_gnn_W2).T, halves(L0_gnn_bm1), halves(L0_gnn_g1), halves(L0_gnn_b1),
                                halves(L0_gnn_m1), halves(L0_gnn_v1), less_than(np.arange(P) % PARTS)], axis=1),
        "wtmp": np.concatenate([halves(np.concatenate([np.asarray(L0_gnn_We1)] * len(WEIGHT_PARTS)
                                                      + [row(L0_gnn_be1)] * PARTS).T),
                                halves(L0_gnn_We2), less_than(part_of)], axis=1),
        "rows": np.concatenate([row(a) for a in (L0_gnn_bm2, L0_gnn_g2, L0_gnn_b2, L0_gnn_m2, L0_gnn_v2, L1_gnn_b1,
                                                 L1_gnn_b2, L0_gnn_be2, L0_gnn_eps)], axis=1),
    }
    nc = bacc.Bacc("TRN2", target_bir_lowering=False, num_devices=1)
    arrays, args = {}, []
    for name, a in data.items():
        arrays[f"in_{name}"] = np.ascontiguousarray(a)
        args.append(nc.dram_tensor(f"in_{name}", a.shape, mybir.dt.from_np(a.dtype), kind="ExternalInput").ap())
    args.append(nc.dram_tensor("out_0", (NODES, D), F32, kind="ExternalOutput").ap())
    args.append(nc.dram_tensor("x1_rows", (ROWS, D), F32, kind="Internal").ap())
    args.append(nc.dram_tensor("residual_rows", (ROWS, D), F32, kind="Internal").ap())
    gnn_kernel(nc, *args)
    result = run_bass_kernel_spmd(nc, [arrays], core_ids=[0])
    return result.results[0]["out_0"]
```
